# Optimizing a Trainium2 kernel written in Bass

```python
import numpy as np
import jax
import jax.numpy as jnp

def _softmax(x, axis=-1):
    return jax.nn.softmax(x, axis=axis)

def _gelu(x):
    return jax.nn.gelu(x, approximate=True)

def _silu(x):
    return jax.nn.silu(x)

def _sigmoid(x):
    return jax.nn.sigmoid(x)

def _layernorm(x, axis=-1, eps=1e-05):
    m = jnp.mean(x, axis=axis, keepdims=True)
    v = jnp.var(x, axis=axis, keepdims=True)
    return (x - m) / jnp.sqrt(v + eps)

def _scatter_add(tgt, idx, src, axis=0):
    return tgt.at[idx].add(src)

def _segment_sum(src, seg, n):
    return jax.ops.segment_sum(src, seg, n)
kernel_name = 'mk_vit_tower_d1_tok_img768_r4_e8acd8'

def setup_inputs(seed: int=0):
    np.random.seed(seed)
    _w = jnp.asarray

    def _rec_inputs():
        import jax
        import jax.numpy as jnp
        _rk = jax.random.key(seed)
        x = -0.000356955 + 1 * jax.random.normal(jax.random.fold_in(_rk, 1), (64, 3, 224, 224), jnp.float32)
        return x
    x = _rec_inputs()

    def _L0_tok_setup():
        import jax, jax.numpy as jnp
        import numpy as np
        P = 16
        PW = P // 2 + 1
        EMBED = 192
        C_IN = 3
        NUM_PATCHES = 196
        key = jax.random.key(seed)
        ks = jax.random.split(key, 7)
        B, H, W = (128, 224, 224)
        in_feat = C_IN * P * PW
        return {'x': jax.random.normal(ks[0], (B, C_IN, H, W), dtype=jnp.float32), 'freq_weight_h': jnp.ones((P,), dtype=jnp.float32), 'freq_weight_w': jnp.ones((PW,), dtype=jnp.float32), 'proj_w': jax.random.normal(ks[1], (EMBED, in_feat), dtype=jnp.float32) / np.sqrt(in_feat), 'proj_b': jnp.zeros((EMBED,), dtype=jnp.float32), 'cls_token': jax.random.normal(ks[2], (1, 1, EMBED), dtype=jnp.float32), 'position_embeddings': jax.random.normal(ks[3], (1, NUM_PATCHES + 1, EMBED), dtype=jnp.float32)}
    _L0_tok_all = _L0_tok_setup()
    _L0_tok_in = {k: v for k, v in _L0_tok_all.items() if k in ('freq_weight_h', 'freq_weight_w', 'proj_w', 'proj_b', 'cls_token', 'position_embeddings')}
    del _L0_tok_all

    def _L0_attn_setup():
        import jax, jax.numpy as jnp
        import numpy as np
        BATCH, L, D, N = (8, 512, 192, 64)
        key = jax.random.key(seed)
        k_u, k_ar, k_ai, k_b, k_c, k_d = jax.random.split(key, 6)
        u = jax.random.normal(k_u, (BATCH, L, D), dtype=jnp.float32)
        A_re = -(0.5 + jax.random.uniform(k_ar, (D, N), dtype=jnp.float32))
        A_im = jax.random.normal(k_ai, (D, N), dtype=jnp.float32)
        B_mat = jax.random.normal(k_b, (D, N), dtype=jnp.float32)
        C_mat = jax.random.normal(k_c, (D, N), dtype=jnp.float32)
        delta = 0.001 + 0.1 * jax.random.uniform(k_d, (D,), dtype=jnp.float32)
        return {'u': u, 'A_re': A_re, 'A_im': A_im, 'B_mat': B_mat, 'C_mat': C_mat, 'delta': delta}
    _L0_attn_all = _L0_attn_setup()
    _L0_attn_in = {k: v for k, v in _L0_attn_all.items() if k in ('A_re', 'A_im', 'B_mat', 'C_mat', 'delta')}
    del _L0_attn_all

    def _L0_ffn_setup():
        import jax, jax.numpy as jnp
        import numpy as np
        B, S, D = (4, 256, 192)
        E = 8
        H = 192
        HS = 768
        TOPK_ROUTED = 2
        key = jax.random.key(seed)
        ks = jax.random.split(key, 10)
        w = lambda k, shape: jax.random.normal(k, shape, dtype=jnp.float32) * 0.02
        return {'x': jax.random.normal(ks[0], (B, S, D), dtype=jnp.float32), 'router_w': w(ks[1], (D, E)), 'w_gate': w(ks[2], (E, D, H)), 'w_up': w(ks[3], (E, D, H)), 'w_down': w(ks[4], (E, H, D)), 'ws_gate': w(ks[5], (D, HS)), 'ws_up': w(ks[6], (D, HS)), 'ws_down': w(ks[7], (HS, D)), 'sg_w': w(ks[8], (D, 1)), 'sg_b': jnp.zeros((1,), jnp.float32)}
    _L0_ffn_all = _L0_ffn_setup()
    _L0_ffn_in = {k: v for k, v in _L0_ffn_all.items() if k in ('router_w', 'w_gate', 'w_up', 'w_down', 'ws_gate', 'ws_up', 'ws_down', 'sg_w', 'sg_b')}
    del _L0_ffn_all
    return {'x': x, 'L0_tok_freq_weight_h': _L0_tok_in['freq_weight_h'], 'L0_tok_freq_weight_w': _L0_tok_in['freq_weight_w'], 'L0_tok_proj_w': _L0_tok_in['proj_w'], 'L0_tok_proj_b': _L0_tok_in['proj_b'], 'L0_tok_cls_token': _L0_tok_in['cls_token'], 'L0_tok_position_embeddings': _L0_tok_in['position_embeddings'], 'L0_attn_A_re': _L0_attn_in['A_re'], 'L0_attn_A_im': _L0_attn_in['A_im'], 'L0_attn_B_mat': _L0_attn_in['B_mat'], 'L0_attn_C_mat': _L0_attn_in['C_mat'], 'L0_attn_delta': _L0_attn_in['delta'], 'L0_ffn_router_w': _L0_ffn_in['router_w'], 'L0_ffn_w_gate': _L0_ffn_in['w_gate'], 'L0_ffn_w_up': _L0_ffn_in['w_up'], 'L0_ffn_w_down': _L0_ffn_in['w_down'], 'L0_ffn_ws_gate': _L0_ffn_in['ws_gate'], 'L0_ffn_ws_up': _L0_ffn_in['ws_up'], 'L0_ffn_ws_down': _L0_ffn_in['ws_down'], 'L0_ffn_sg_w': _L0_ffn_in['sg_w'], 'L0_ffn_sg_b': _L0_ffn_in['sg_b']}

def reference(x, L0_tok_freq_weight_h, L0_tok_freq_weight_w, L0_tok_proj_w, L0_tok_proj_b, L0_tok_cls_token, L0_tok_position_embeddings, L0_attn_A_re, L0_attn_A_im, L0_attn_B_mat, L0_attn_C_mat, L0_attn_delta, L0_ffn_router_w, L0_ffn_w_gate, L0_ffn_w_up, L0_ffn_w_down, L0_ffn_ws_gate, L0_ffn_ws_up, L0_ffn_ws_down, L0_ffn_sg_w, L0_ffn_sg_b):
    import jax
    import jax.numpy as jnp

    def _L0_tok_ref(x, freq_weight_h, freq_weight_w, proj_w, proj_b, cls_token, position_embeddings):
        import jax, jax.numpy as jnp
        import numpy as np
        P = 16
        PW = P // 2 + 1
        EMBED = 192
        C_IN = 3
        NUM_PATCHES = 196
        B, C, H, W = x.shape
        nH, nW = (H // P, W // P)
        N = nH * nW
        xp = x.reshape(B, C, nH, P, nW, P).transpose(0, 1, 2, 4, 3, 5).reshape(B, C, N, P, P)
        xf = jnp.fft.rfft2(xp, norm='ortho').real
        xf = xf * freq_weight_h[:, None] * freq_weight_w[None, :]
        xf = xf.transpose(0, 2, 1, 3, 4).reshape(B, N, C * P * PW)
        x_proj = xf @ proj_w.T + proj_b
        cls = jnp.broadcast_to(cls_token, (B, 1, EMBED))
        out = jnp.concatenate([cls, x_proj], axis=1) + position_embeddings
        return out

    def _L0_attn_ref(u, A_re, A_im, B_mat, C_mat, delta):
        import jax, jax.numpy as jnp
        import numpy as np
        BATCH, L, D, N = (8, 512, 192, 64)
        A = (A_re + 1j * A_im).astype(jnp.complex64)
        dA = delta[:, None].astype(jnp.complex64) * A
        A_bar = jnp.exp(dA)
        B_bar = (A_bar - 1.0) / A * B_mat.astype(jnp.complex64)
        seq_len = u.shape[1]
        ell = jnp.arange(seq_len, dtype=jnp.float32)
        vand = jnp.exp(dA[:, :, None] * ell[None, None, :])
        coef = C_mat.astype(jnp.complex64) * B_bar
        K = jnp.einsum('dn,dnl->dl', coef, vand)
        nfft = 2 * seq_len
        Kf = jnp.fft.fft(K, n=nfft, axis=-1)
        u_dl = jnp.transpose(u, (0, 2, 1)).astype(jnp.complex64)
        uf = jnp.fft.fft(u_dl, n=nfft, axis=-1)
        y = jnp.fft.ifft(uf * Kf[None, :, :], axis=-1)[..., :seq_len].real
        return jnp.transpose(y, (0, 2, 1))

    def _L0_ffn_ref(x, router_w, w_gate, w_up, w_down, ws_gate, ws_up, ws_down, sg_w, sg_b):
        import jax, jax.numpy as jnp
        import numpy as np
        B, S, D = (4, 256, 192)
        E = 8
        H = 192
        HS = 768
        TOPK_ROUTED = 2
        probs = jax.nn.softmax(x @ router_w, axis=-1)
        gates, idx = jax.lax.top_k(probs, TOPK_ROUTED)
        gates = gates / jnp.sum(gates, axis=-1, keepdims=True)
        n_exp = router_w.shape[1]
        dense_g = jnp.sum(jax.nn.one_hot(idx, n_exp, dtype=x.dtype) * gates[..., None], axis=-2)
        g = jax.nn.silu(jnp.einsum('bsd,edh->bseh', x, w_gate))
        u = jnp.einsum('bsd,edh->bseh', x, w_up)
        expert_out = jnp.einsum('bseh,ehd->bsed', g * u, w_down)
        routed = jnp.einsum('bse,bsed->bsd', dense_g, expert_out)
        shared = jax.nn.silu(x @ ws_gate) * (x @ ws_up) @ ws_down
        alpha = jax.nn.sigmoid(x @ sg_w + sg_b)
        return alpha * shared + (1.0 - alpha) * routed
    h = _L0_tok_ref(x, L0_tok_freq_weight_h, L0_tok_freq_weight_w, L0_tok_proj_w, L0_tok_proj_b, L0_tok_cls_token, L0_tok_position_embeddings)
    h = h + _L0_attn_ref(_layernorm(h, axis=-1), L0_attn_A_re, L0_attn_A_im, L0_attn_B_mat, L0_attn_C_mat, L0_attn_delta)
    h = h + _L0_ffn_ref(_layernorm(h, axis=-1), L0_ffn_router_w, L0_ffn_w_gate, L0_ffn_w_up, L0_ffn_w_down, L0_ffn_ws_gate, L0_ffn_ws_up, L0_ffn_ws_down, L0_ffn_sg_w, L0_ffn_sg_b)
    return h

_drawn_inputs = setup_inputs


def setup_inputs(seed=0):
    import zlib

    import numpy as np

    out = dict(_drawn_inputs(seed))
    spreads = {'L0_tok_freq_weight_h': (1.0, 0.2),
     'L0_tok_freq_weight_w': (1.0, 0.2),
     'L0_tok_proj_b': (0.0, 0.1)}
    factors = {'L0_ffn_router_w': 8.0,
     'L0_ffn_w_gate': 8.0,
     'L0_ffn_w_up': 8.0,
     'L0_ffn_w_down': 8.0,
     'L0_ffn_ws_gate': 8.0,
     'L0_ffn_ws_up': 8.0,
     'L0_ffn_ws_down': 8.0,
     'L0_ffn_sg_w': 8.0}
    for name, (base, spread) in spreads.items():
        noise = np.random.default_rng([zlib.crc32(name.encode()), seed]).standard_normal(out[name].shape)
        drawn = base * np.exp(spread * noise) if base else spread * noise
        out[name] = jnp.asarray(drawn.astype(out[name].dtype))
    for name, factor in factors.items():
        out[name] = (out[name] * factor).astype(out[name].dtype)
    return out
```

```python
from contextlib import ExitStack

import numpy as np
import concourse.bass as bass
from concourse import mybir

F32 = mybir.dt.float32
F16 = mybir.dt.float16
U32 = mybir.dt.uint32
ALU = mybir.AluOpType
ACT = mybir.ActivationFunctionType

B, C, IMG, P = 64, 3, 224, 16
SIDE = IMG // P
NPATCH = SIDE * SIDE
HALF = NPATCH // 2
SEQ = NPATCH + 1
D = 192
DH = D // 2
KH, KW = P, P // 2 + 1
NFREQ = KH * KW
FCH = NFREQ // 2
NST = 64
E, HE, HS = 8, 192, 768
EPS = 1e-5
SCALE = 16.0

GI = 4
NG = B // GI
GT = GI * NPATCH
ROWS = 128
NX = 18

KA, KB = 15, 14
KL = KA * KB
CG = 8
NCG = D // CG
TC = NPATCH
DQ = DH // 2
SKIP = KL - SEQ
RW = SKIP + 1 + HALF + TC

NTOK = B * SEQ
BT, NT = 512, 4
LAST_NT = 3
NBLK = NTOK // BT + 1
LAST_START = NTOK - LAST_NT * 128
HID = HS + E * HE
NCH = HID // 128
NSH = HS // 128
NRO = NCH - NSH
XW = 2 * D


def pixel_fold():
    pairs, selfs = [], []
    for r in range(P):
        for s in range(P):
            q = ((-r) % P, (-s) % P)
            if q == (r, s):
                selfs.append((r, s))
            elif (r, s) < q:
                pairs.append(((r, s), q))
    first = [p for p, _ in pairs] + selfs[:2]
    second = [q for _, q in pairs] + selfs[:2]
    return first, second, len(pairs), selfs[2:]


def dft_constants():
    first, _, npairs, rest = pixel_fold()
    kh, kw = np.meshgrid(np.arange(KH), np.arange(KW), indexing="ij")
    kh, kw = kh.reshape(-1), kw.reshape(-1)

    def col(p):
        return np.cos(2 * np.pi * ((kh * p[0] + kw * p[1]) % P) / P) / P

    fa = np.stack([col(p) * (1.0 if n < npairs else 0.5) for n, p in enumerate(first)], 1)
    fx = np.zeros((NFREQ, C, NX))
    for c in range(C):
        for rep in range(3):
            for k, p in enumerate(rest):
                fx[:, c, rep * 6 + c * 2 + k] = col(p)
    fa = fa.reshape(2, FCH, ROWS).transpose(1, 0, 2)
    fx = fx.reshape(2, FCH, C, NX).transpose(1, 0, 2, 3)
    return np.ascontiguousarray(fa, np.float32), np.ascontiguousarray(fx, np.float32)


def prepare(nc, io, u, w, scratch):
    taps, resid, mixed = scratch
    with ExitStack() as ctx:
        def sb(name, shape, dt=F32):
            return ctx.enter_context(nc.sbuf_tensor(name, shape, dt))

        def sem(name):
            return ctx.enter_context(nc.semaphore(name))

        fa = sb("fa", [FCH, 2, ROWS])
        fx = sb("fx", [FCH, 2, C, NX])
        pw = sb("pw", [FCH, 2, C, D])
        freq = sb("freq", [FCH, 2, 2])
        fw = sb("fw", [FCH, 2])
        pws = sb("pws", [FCH, 2, C, D])
        wf = sb("wf", [ROWS, C, D])
        wxf = sb("wxf", [NX, D])
        wxh = sb("wxh", [NX, D], F16)
        ssm = sb("ssm", [128, 5, DH])
        v = sb("v", [128, 2, DH])
        p = sb("p", [128, 2, DH])
        e1 = sb("e1", [128, 2, DH])
        cf = sb("cf", [128, 2, DH])
        q = sb("q", [128, 4, DH])
        sr = sb("sr", [128, 2, KA, DH])
        si = sb("si", [128, 2, KA, DH])
        tq = sb("tq", [128, 2, KA, DH])
        tp = sb("tp", [128, 2, KA, DH])
        zq = sb("zq", [128, 2, KB, DH])
        zp = sb("zp", [128, 2, DH, KA])
        kf = sr[0:CG * KA].rearrange("p k a d -> p (k a d)")[:, 0:NCG * CG * KB].rearrange(
            "p (g c) -> p g c", g=NCG)
        ks = si[0:CG * KA].rearrange("p k a d -> p (k a d)")[:, 0:NCG * CG * KB].bitcast(F16).rearrange(
            "p (g c k) -> p g c k", g=NCG, k=2)
        zero = sb("zero", [DH, 2 * (RW - KL)], F16)
        cl = sb("cl", [3, 2, D])
        hc = sb("hc", [3, D])
        cst = sb("cst", [3, 6])
        cmv = sb("cmv", [3, 2])
        cve = sb("cve", [3, 1])
        crs = sb("crs", [3, 1])
        chalf = sb("chalf", [3, 1])
        uc = sb("uc", [3, D])
        ucs = sb("ucs", [3, D, 2], F16)
        k0 = sb("k0", [1, D, 2], F16)
        k0f = sb("k0f", [1, D])
        yc = sb("yc", [1, D])
        psw = ctx.enter_context(nc.psum_tensor("psw", [128, 2, 512], F32))
        psk = ctx.enter_context(nc.psum_tensor("psk", [128, 6, 512], F32))

        loaded_w, loaded_a, loaded_c = sem("loaded_w"), sem("loaded_a"), sem("loaded_c")
        d = sem("vector_done")
        pws_ready, wps_ready, powers_ready, taps_ready = (
            sem("pws_ready"), sem("wps_ready"), sem("powers_ready"), sem("taps_ready"))
        zero_ready, split_ready, hc_ready, cmv_ready = (
            sem("zero_ready"), sem("split_ready"), sem("hc_ready"), sem("cmv_ready"))
        g, crs_ready, ucs_ready, rep_done = sem("gp"), sem("crs_ready"), sem("ucs_ready"), sem("rep_done")
        taps_out, k0_in, yc_ready, out_done = sem("taps_out"), sem("k0_in"), sem("yc_ready"), sem("out_done")

        block = ctx.enter_context(nc.Block())

        @block.sync
        def _(sp):
            for dst, src in ((fa, "fa"), (fx, "fx"), (pw, "pw"), (freq, "freq")):
                sp.dma_start(dst[:], io[src][:]).then_inc(loaded_w, 16)
            sp.dma_start(ssm[:], io["ssm"][:]).then_inc(loaded_a, 16)
            sp.dma_start(cl[:], io["cls"][:]).then_inc(loaded_c, 16)
            sp.wait_ge(zero_ready, 1)
            for n in range(2):
                rows = taps[n * DH:(n + 1) * DH]
                sp.dma_start(rows[:, KL:RW, :].rearrange("r c k -> r (c k)"), zero[:]).then_inc(taps_out, 16)
            sp.wait_ge(split_ready, 1)
            for i in range(CG):
                dst = bass.AP(taps.tensor, i * RW * 2,
                              [(2 * KB, KA), (CG * RW * 2, NCG), (1, 2 * KB)])
                src = ks[i * KA:(i + 1) * KA, :, i * KB:(i + 1) * KB, :].rearrange("a g b k -> a g (b k)")
                sp.dma_start(dst, src).then_inc(taps_out, 16)
            sp.wait_ge(taps_out, 16 * (2 + CG))
            with nc.allow_non_contiguous_dma(reason="one tap of each channel"):
                for n in range(2):
                    for q in range(2):
                        rows = taps[n * DH:(n + 1) * DH, KL - 1, :].rearrange("(g q c) k -> q g c k", q=2, c=CG // 2)
                        dst = k0[:, n * DH + q * DQ:n * DH + (q + 1) * DQ, :]
                        sp.dma_start(dst.rearrange("p (g c) k -> p g c k", c=CG // 2),
                                     rows[q:q + 1]).then_inc(k0_in, 16)
            sp.wait_ge(hc_ready, 1)
            sp.dma_start(resid.rearrange("(b l) d -> l b d", l=SEQ)[0:1],
                         hc[0:1, :].unsqueeze(1).to_broadcast([1, B, D])).then_inc(out_done, 16)
            sp.wait_ge(yc_ready, 1)
            sp.dma_start(mixed.rearrange("(b l) d -> l b d", l=SEQ)[0:1],
                         yc[0:1, :].unsqueeze(1).to_broadcast([1, B, D])).then_inc(out_done, 16)
            sp.wait_ge(out_done, 32)

        @block.gpsimd
        def _(pool):
            nc.gpsimd.memset(zero[:], 0.0).then_inc(zero_ready, 1)
            nc.gpsimd.memset(chalf[:], -0.5).then_inc(g, 1)
            pool.wait_ge(cmv_ready, 1)
            nc.gpsimd.tensor_scalar(cve[:], cmv[:, 1:2], EPS, None, ALU.add).then_inc(g, 1)
            pool.wait_ge(g, 2)
            nc.gpsimd.tensor_tensor(crs[:], cve[:], chalf[:], ALU.pow).then_inc(crs_ready, 1)

        @block.scalar
        def _(act):
            act.wait_ge(ucs_ready, 1)
            for h in range(2):
                src = ucs[:, h * DH:(h + 1) * DH, :].unsqueeze(3).to_broadcast([3, DH, 2, B])
                last = nc.scalar.copy(u[h][96:99, 0], src)
            last.then_inc(rep_done, 1)

        @block.tensor
        def _(pe):
            pe.wait_ge(pws_ready, 1)
            for c in range(C):
                for k in range(2):
                    nc.tensor.matmul(psw[:, c // 2, (c % 2) * D:(c % 2 + 1) * D], fa[:, k, :], pws[:, k, c, :],
                                     start=(k == 0), stop=(k == 1))
            for c in range(C):
                for k in range(2):
                    last = nc.tensor.matmul(psw[0:NX, 1, D:2 * D], fx[:, k, c, :], pws[:, k, c, :],
                                            start=(c == 0 and k == 0), stop=(c == C - 1 and k == 1))
            last.then_inc(wps_ready, 1)
            pe.wait_ge(powers_ready, 1)
            for G in range(NCG):
                h, n = divmod(G, NCG // 2)
                part = slice(h * NST, (h + 1) * NST)
                for k in range(2):
                    last = nc.tensor.matmul(
                        psk[0:CG * KA, h * 3 + n // 4, (n % 4) * CG * KB:(n % 4 + 1) * CG * KB],
                        zp[part, k, n * CG:(n + 1) * CG].rearrange("n d a -> n (d a)"),
                        zq[part, k, :, n * CG:(n + 1) * CG].rearrange("n b d -> n d b"),
                        start=(k == 0), stop=(k == 1))
            last.then_inc(taps_ready, 1)

        @block.vector
        def _(dve):
            n = [0]

            def step(ins):
                n[0] += 1
                ins.then_inc(d, 1)
                dve.wait_ge(d, n[0])

            def tt(o, a, b, op):
                step(nc.vector.tensor_tensor(o, a, b, op))

            dve.wait_ge(loaded_w, 64)
            tt(fw[:], freq[:, 0], freq[:, 1], ALU.mult)
            nc.vector.tensor_tensor(pws[:], pw[:], fw[:].unsqueeze(2).unsqueeze(3).to_broadcast([FCH, 2, C, D]),
                                    ALU.mult).then_inc(pws_ready, 1)

            dve.wait_ge(loaded_c, 16)
            nc.vector.tensor_tensor(hc[:], cl[:, 0], cl[:, 1], ALU.add).then_inc(hc_ready, 1)
            dve.wait_ge(hc_ready, 1)
            step(nc.vector.bn_stats(cst[:], hc[:]))
            nc.vector.bn_aggr(cmv[:], cst[:]).then_inc(cmv_ready, 1)

            dve.wait_ge(loaded_a, 16)
            are, aim, bm, cm, dl = (ssm[:, i] for i in range(5))
            tt(v[:, 0], are, dl, ALU.mult)
            tt(v[:, 1], aim, dl, ALU.mult)
            step(nc.vector.tensor_scalar(v[:], v[:], 1.0 / 16, None, ALU.mult))

            def cmul(o, a, b):
                nc.vector.tensor_tensor(q[:, 0:2], a[:, 0:1].to_broadcast([128, 2, DH]), b, ALU.mult)
                tt(q[:, 2:4], a[:, 1:2].to_broadcast([128, 2, DH]), b, ALU.mult)
                nc.vector.tensor_tensor(o[:, 0], q[:, 0], q[:, 3], ALU.subtract)
                tt(o[:, 1], q[:, 1], q[:, 2], ALU.add)

            order = 8
            step(nc.vector.tensor_scalar(p[:], v[:], 1.0 / order, None, ALU.mult))
            step(nc.vector.tensor_scalar(p[:, 0], p[:, 0], 1.0, None, ALU.add))
            for k in range(order - 1, 1, -1):
                cmul(p, v, p[:])
                step(nc.vector.tensor_scalar(p[:], p[:], 1.0 / k, None, ALU.mult))
                step(nc.vector.tensor_scalar(p[:, 0], p[:, 0], 1.0, None, ALU.add))
            cmul(e1, v, p[:])
            for _ in range(4):
                nc.vector.tensor_scalar(p[:, 0], e1[:, 0], 2.0, None, ALU.add)
                step(nc.vector.tensor_copy(p[:, 1], e1[:, 1]))
                cmul(e1, e1, p[:])

            nc.vector.tensor_tensor(q[:, 0], are, are, ALU.mult)
            tt(q[:, 1], aim, aim, ALU.mult)
            tt(q[:, 2], q[:, 0], q[:, 1], ALU.add)
            nc.vector.reciprocal(q[:, 3], q[:, 2])
            tt(q[:, 0], bm, cm, ALU.mult)
            step(nc.vector.scalar_tensor_tensor(out=v[:, 0], in0=q[:, 0], scalar=SCALE, in1=q[:, 3],
                                                op0=ALU.mult, op1=ALU.mult))
            nc.vector.tensor_tensor(q[:, 0], e1[:, 0], are, ALU.mult)
            nc.vector.tensor_tensor(q[:, 1], e1[:, 1], aim, ALU.mult)
            nc.vector.tensor_tensor(q[:, 2], e1[:, 1], are, ALU.mult)
            tt(q[:, 3], e1[:, 0], aim, ALU.mult)
            nc.vector.tensor_tensor(q[:, 0], q[:, 0], q[:, 1], ALU.add)
            tt(q[:, 2], q[:, 2], q[:, 3], ALU.subtract)
            nc.vector.tensor_tensor(cf[:, 0], q[:, 0], v[:, 0], ALU.mult)
            tt(cf[:, 1], q[:, 2], v[:, 0], ALU.mult)

            def powers(t, first):
                nc.vector.memset(t[:, :, 0], 0.0)
                step(nc.vector.tensor_copy(t[:, :, 1], first))
                for m, c in ((1, 1), (2, 2), (4, 4), (8, 6)):
                    low, new = t[:, :, 1:1 + c], t[:, :, m + 1:m + 1 + c]
                    shape = [128, 2, c, DH]
                    nc.vector.tensor_tensor(sr[:, :, 0:c], t[:, 0:1, m:m + 1].to_broadcast(shape), low, ALU.mult)
                    nc.vector.tensor_tensor(si[:, :, 0:c], t[:, 1:2, m:m + 1].to_broadcast(shape), low, ALU.mult)
                    tt(new, t[:, :, m:m + 1].to_broadcast(shape), low, ALU.add)
                    tt(new, new, sr[:, :, 0:c], ALU.add)
                    nc.vector.tensor_tensor(new[:, 0], new[:, 0], si[:, 1, 0:c], ALU.subtract)
                    tt(new[:, 1], new[:, 1], si[:, 0, 0:c], ALU.add)

            powers(tq, e1[:])
            powers(tp, tq[:, :, KB])
            nc.vector.tensor_scalar(zq[:, 0], tq[:, 0, KB - 1::-1], 1.0, None, ALU.add)
            nc.vector.tensor_copy(zq[:, 1], tq[:, 1, KB - 1::-1])
            step(nc.vector.tensor_scalar(tp[:, 0], tp[:, 0], 1.0, None, ALU.add))
            shape = [128, 2, KA, DH]
            nc.vector.tensor_tensor(sr[:], cf[:, 0:1].unsqueeze(1).to_broadcast(shape), tp[:], ALU.mult)
            tt(si[:], cf[:, 1:2].unsqueeze(1).to_broadcast(shape), tp[:], ALU.mult)
            nc.vector.tensor_tensor(zp[:, 0].rearrange("p d a -> p a d"), sr[:, 0, ::-1], si[:, 1, ::-1], ALU.subtract)
            nc.vector.scalar_tensor_tensor(out=zp[:, 1].rearrange("p d a -> p a d"), in0=sr[:, 1, ::-1], scalar=-1.0, in1=si[:, 0, ::-1],
                                           op0=ALU.mult, op1=ALU.subtract).then_inc(powers_ready, 1)

            dve.wait_ge(crs_ready, 1)
            step(nc.vector.tensor_scalar(uc[:], hc[:], cmv[:, 0:1], crs[:], ALU.subtract, ALU.mult))
            step(nc.vector.tensor_copy(ucs[:, :, 0], uc[:]))
            nc.vector.tensor_tensor(ucs[:, :, 1], uc[:], ucs[:, :, 0], ALU.subtract).then_inc(ucs_ready, 1)
            dve.wait_ge(wps_ready, 1)
            nc.vector.tensor_scalar(wf[:, 0:2], psw[:, 0, 0:2 * D].rearrange("p (c e) -> p c e", c=2), SCALE, None,
                                    ALU.mult)
            nc.vector.tensor_scalar(wf[:, 2], psw[:, 1, 0:D], SCALE, None, ALU.mult)
            step(nc.vector.tensor_scalar(wxf[:], psw[0:NX, 1, D:2 * D], SCALE, None, ALU.mult))
            nc.vector.tensor_copy(w["hi"][:], wf[:])
            step(nc.vector.tensor_copy(wxh[:], wxf[:]))
            nc.vector.tensor_tensor(w["lo"][:], wf[:], w["hi"][:], ALU.subtract)
            step(nc.vector.scalar_tensor_tensor(out=w["x"][:], in0=wxh[:], scalar=w["signs"][:, 0:1], in1=wxf[:],
                                                op0=ALU.mult, op1=ALU.add))

            dve.wait_ge(taps_ready, 1)
            kfv = kf.rearrange("p g c -> p (g c)").rearrange("p (k c) -> p k c", k=6)
            step(nc.vector.tensor_copy(kfv, psk[0:CG * KA, :, 0:4 * CG * KB]))
            step(nc.vector.tensor_copy(ks[:, :, :, 0], kf))
            nc.vector.tensor_tensor(ks[:, :, :, 1], kf, ks[:, :, :, 0], ALU.subtract).then_inc(split_ready, 1)

            dve.wait_ge(k0_in, 64)
            tt(k0f[:], k0[:, :, 0], k0[:, :, 1], ALU.add)
            nc.vector.scalar_tensor_tensor(out=yc[:], in0=k0f[:], scalar=1.0 / SCALE, in1=uc[0:1, :],
                                           op0=ALU.mult, op1=ALU.mult).then_inc(yc_ready, 1)


def embed(nc, io, u, w, resid):
    with ExitStack() as ctx:
        def sb(name, shape, dt=F32):
            return ctx.enter_context(nc.sbuf_tensor(name, shape, dt))

        def sem(name):
            return ctx.enter_context(nc.semaphore(name))

        xa = [sb(f"xa{i}", [ROWS, C, GT]) for i in range(2)]
        xb = [sb(f"xb{i}", [ROWS, C, GT]) for i in range(2)]
        xe = [sb(f"xe{i}", [NX, GT]) for i in range(2)]
        xh = [sb(f"xh{i}", [ROWS, C, GT], F16) for i in range(2)]
        xl = [sb(f"xl{i}", [ROWS, C, GT], F16) for i in range(2)]
        eh = [sb(f"eh{i}", [NX, GT], F16) for i in range(2)]
        es = [sb(f"es{i}", [NX, GT], F16) for i in range(2)]
        add = sb("add", [HALF, 2, D])
        pos = sb("pos", [HALF, 2, D])
        h = [sb(f"h{i}", [HALF, GI, 2, D]) for i in range(2)]
        un = sb("un", [HALF, GI, 2, D])
        uh = sb("uh", [HALF, GI, 2, D], F16)
        st = sb("st", [HALF, GI * 2, 6])
        mv = sb("mv", [HALF, GI * 2, 2])
        ve = sb("ve", [HALF, GI * 2, 1])
        rs = sb("rs", [HALF, GI * 2, 1])
        mhalf = sb("mhalf", [HALF, GI * 2, 1])
        eps = sb("eps", [HALF, GI * 2, 1])
        ps = ctx.enter_context(nc.psum_tensor("ps", [HALF, 2 * GI, 512], F32))

        names = ("x_in0", "x_in1", "pos_in", "folded", "xh_ready", "xl_ready", "eh_ready", "es_ready", "tokens_ready",
                 "h_ready", "stats_ready", "mv_ready", "ve_ready", "rs_ready", "const_ready", "un_ready",
                 "uh_ready", "ul_done", "u_copied", "h_out0", "h_out1", "add_ready")
        s = {name: sem(name) for name in names}
        block = ctx.enter_context(nc.Block())
        PAIRS = NG // 2

        @block.sync
        def _(sp):
            sp.dma_start(add[:], io["pos"][0]).then_inc(s["pos_in"], 16)
            sp.dma_start(pos[:], io["pos"][1]).then_inc(s["pos_in"], 16)

            def load(g, i, wait):
                if wait:
                    sp.wait_ge(s["xl_ready"], g - 1)
                    sp.wait_ge(s["es_ready"], g - 1)
                sp.dma_start(xa[i][:], io["xa"][bass.ds(g, 1)].rearrange("g p c t -> (g p) c t")).then_inc(s[f"x_in{i}"], 16)
                sp.dma_start(xb[i][:], io["xb"][bass.ds(g, 1)].rearrange("g p c t -> (g p) c t")).then_inc(s[f"x_in{i}"], 16)
                sp.dma_start(xe[i][:], io["xe"][bass.ds(g, 1)].rearrange("g p t -> (g p) t")).then_inc(s[f"x_in{i}"], 16)

            for i in range(2):
                load(i, i, False)
            with sp.Fori(1, PAIRS) as j:
                for i in range(2):
                    load(2 * j + i, i, True)

        @block.scalar
        def _(act):
            def split(g, i):
                act.wait_ge(s["folded"], g + 1)
                nc.scalar.copy(xh[i][:], xa[i][:]).then_inc(s["xh_ready"], 1)
                nc.scalar.copy(eh[i][:], xe[i][:]).then_inc(s["eh_ready"], 1)

            def store(g, i, guarded):
                act.wait_ge(s["h_ready"], GI * (g + 1))
                rows = resid.rearrange("(b l) d -> b l d", l=SEQ)[bass.ds(GI * g, GI), 1:SEQ]
                for k in range(2):
                    act.dma_start(rows[:, k * HALF:(k + 1) * HALF].rearrange("b l d -> l b d"),
                                  h[i][:, :, k]).then_inc(s[f"h_out{i}"], 16)
                act.wait_ge(s["un_ready"], g + 1)
                if guarded:
                    act.wait_ge(s["ul_done"], 4 * g)
                    act.wait_ge(s["u_copied"], 4 * g)
                nc.scalar.copy(uh[:], un[:]).then_inc(s["uh_ready"], 1)
                act.wait_ge(s["uh_ready"], g + 1)
                for n in range(2):
                    for k in range(2):
                        nc.scalar.copy(u[n][0:HALF, k, :, 0, bass.ds(GI * g, GI)],
                                       uh[:, :, k, n * DH:(n + 1) * DH].rearrange("p b d -> p d b")
                                       ).then_inc(s["u_copied"], 1)

            def group(g, i, first=False):
                if g is not first and not first:
                    act.wait_ge(s["tokens_ready"], GI * (g - 1))
                split(g, i)

            split(0, 0)
            split(1, 1)
            store(0, 0, False)
            with act.Fori(1, PAIRS) as j:
                for i in range(2):
                    g = 2 * j + i
                    act.wait_ge(s["tokens_ready"], GI * (g - 1))
                    split(g, i)
                    store(g - 1, 1 - i, True)
            store(NG - 1, 1, True)
            for i in range(2):
                act.wait_ge(s[f"h_out{i}"], 16 * NG + 16)

        @block.gpsimd
        def _(pool):
            nc.gpsimd.memset(mhalf[:], -0.5).then_inc(s["const_ready"], 1)
            nc.gpsimd.memset(eps[:], EPS).then_inc(s["const_ready"], 1)
            pool.wait_ge(s["const_ready"], 2)

            def low(g, i):
                pool.wait_ge(s["xh_ready"], g + 1)
                nc.gpsimd.tensor_tensor(xl[i][:], xa[i][:], xh[i][:], ALU.subtract).then_inc(s["xl_ready"], 1)

            def rstd(g):
                pool.wait_ge(s["mv_ready"], g + 1)
                nc.gpsimd.tensor_tensor(ve[:], mv[:, :, 1:2], eps[:], ALU.add).then_inc(s["ve_ready"], 1)
                pool.wait_ge(s["ve_ready"], g + 1)
                nc.gpsimd.tensor_tensor(rs[:], ve[:], mhalf[:], ALU.pow).then_inc(s["rs_ready"], 1)

            low(0, 0)
            low(1, 1)
            rstd(0)
            with pool.Fori(1, PAIRS) as j:
                for i in range(2):
                    low(2 * j + i, i)
                    rstd(2 * j + i - 1)
            rstd(NG - 1)

        @block.tensor
        def _(pe):
            def tokens(g, i, guarded):
                pe.wait_ge(s["xl_ready"], g + 1)
                pe.wait_ge(s["es_ready"], g + 1)
                for m in range(GI):
                    bank = GI * i + m
                    if guarded:
                        pe.wait_ge(s["h_ready"], GI * (g - 2) + m + 1)
                    for k in range(2):
                        out = ps[:, bank, k * D:(k + 1) * D]
                        t = slice((2 * m + k) * HALF, (2 * m + k + 1) * HALF)
                        nc.tensor.matmul(out, es[i][:, t], w["x"][:], start=True, stop=False)
                        for c in range(C):
                            nc.tensor.matmul(out, xh[i][:, c, t], w["hi"][:, c], start=False, stop=False)
                            nc.tensor.matmul(out, xh[i][:, c, t], w["lo"][:, c], start=False, stop=False)
                            last = nc.tensor.matmul(out, xl[i][:, c, t], w["hi"][:, c], start=False, stop=(c == C - 1))
                    last.then_inc(s["tokens_ready"], 1)

            for i in range(2):
                tokens(i, i, False)
            with pe.Fori(1, PAIRS) as j:
                for i in range(2):
                    tokens(2 * j + i, i, True)

        @block.vector
        def _(dve):
            dve.wait_ge(s["pos_in"], 32)
            nc.vector.tensor_tensor(add[:], add[:], pos[:], ALU.add).then_inc(s["add_ready"], 1)
            dve.wait_ge(s["add_ready"], 1)

            def fold(g, i):
                dve.wait_ge(s[f"x_in{i}"], 24 * (g - i) + 48)
                nc.vector.tensor_tensor(xa[i][:], xa[i][:], xb[i][:], ALU.add).then_inc(s["folded"], 1)

            def low_rows(g, i):
                dve.wait_ge(s["eh_ready"], g + 1)
                nc.vector.scalar_tensor_tensor(out=es[i][:], in0=eh[i][:], scalar=w["signs"][:, 1:2], in1=xe[i][:],
                                               op0=ALU.mult, op1=ALU.add).then_inc(s["es_ready"], 1)

            def finish(g, i, guarded):
                if guarded:
                    dve.wait_ge(s[f"h_out{i}"], 16 * (g - i) + 16)
                for m in range(GI):
                    dve.wait_ge(s["tokens_ready"], GI * g + m + 1)
                    nc.vector.scalar_tensor_tensor(
                        out=h[i][:, m].rearrange("p k d -> p (k d)"), in0=ps[:, GI * i + m, 0:2 * D],
                        scalar=1.0 / SCALE, in1=add[:].rearrange("p k d -> p (k d)"),
                        op0=ALU.mult, op1=ALU.add).then_inc(s["h_ready"], 1)
                dve.wait_ge(s["h_ready"], GI * (g + 1))
                for n in range(2 * GI):
                    last = nc.vector.bn_stats(st[:, n], h[i][:, n // 2, n % 2])
                last.then_inc(s["stats_ready"], 1)
                dve.wait_ge(s["pos_in"], 32)
                dve.wait_ge(s["stats_ready"], g + 1)
                for n in range(2 * GI):
                    last = nc.vector.bn_aggr(mv[:, n], st[:, n])
                last.then_inc(s["mv_ready"], 1)

            def normal(g, i):
                dve.wait_ge(s["rs_ready"], g + 1)
                for n in range(2 * GI):
                    last = nc.vector.tensor_scalar(un[:, n // 2, n % 2], h[i][:, n // 2, n % 2], mv[:, n, 0:1],
                                                   rs[:, n], ALU.subtract, ALU.mult)
                last.then_inc(s["un_ready"], 1)

            def low_u(g):
                dve.wait_ge(s["uh_ready"], g + 1)
                for n in range(2):
                    for k in range(2):
                        nc.vector.tensor_tensor(u[n][0:HALF, k, :, 1, bass.ds(GI * g, GI)],
                                                un[:, :, k, n * DH:(n + 1) * DH].rearrange("p b d -> p d b"),
                                                uh[:, :, k, n * DH:(n + 1) * DH].rearrange("p b d -> p d b"),
                                                ALU.subtract).then_inc(s["ul_done"], 1)

            for i in range(2):
                dve.sem_inc(s[f"h_out{i}"], 16)
            fold(0, 0)
            low_rows(0, 0)
            fold(1, 1)
            low_rows(1, 1)
            finish(0, 0, False)
            normal(0, 0)
            with dve.Fori(1, PAIRS) as j:
                for i in range(2):
                    g = 2 * j + i
                    fold(g, i)
                    low_u(g - 2)
                    low_rows(g, i)
                    finish(g - 1, 1 - i, True)
                    dve.wait_ge(s["u_copied"], 4 * (g - 1))
                    normal(g - 1, 1 - i)
            low_u(NG - 2)
            finish(NG - 1, 1, True)
            normal(NG - 1, 1)
            low_u(NG - 1)


def mix(nc, u, taps, mixed):
    with ExitStack() as ctx:
        def sb(name, shape, dt=F32):
            return ctx.enter_context(nc.sbuf_tensor(name, shape, dt))

        def sem(name):
            return ctx.enter_context(nc.semaphore(name))

        CQ = CG // 2
        t = [sb(f"toeplitz{i}", [HALF + 1, 2, CQ, TC, 2], F16) for i in range(2)]
        ug = [sb(f"ug{i}", [HALF + 1, 2, 2, CQ, 2, B], F16) for i in range(2)]
        y = sb("y", [128, NPATCH, DQ])
        ps = ctx.enter_context(nc.psum_tensor("conv", [128, 4, 512], F32))
        names = ("t_in0", "t_in1", "u_ready", "u2_ready", "conv0", "conv1", "y0", "y1", "y_out")
        t_in0, t_in1, u_ready, u2_ready, conv0, conv1, y0, y1, y_out = (sem(n) for n in names)
        block = ctx.enter_context(nc.Block())
        HG = NCG // 2
        t_in = (t_in0, t_in1)

        @block.sync
        def _(sp):
            def load(n, i, guarded):
                if guarded:
                    sp.wait_ge(conv1, n - 1)
                sp.dma_start(t[i][0:HALF].rearrange("p q c t k -> p (q c) (t k)"),
                             bass.AP(taps.tensor, n * (CG * RW * 2) + 2 * (SKIP + 1),
                                     [(2, HALF), (RW * 2, CG), (1, TC * 2)])).then_inc(t_in[i], 16)
                sp.dma_start(t[i][HALF:HALF + 1].rearrange("p q c t k -> p (q c) (t k)"),
                             bass.AP(taps.tensor, n * (CG * RW * 2) + 2 * SKIP,
                                     [(RW * 2 * D, 1), (RW * 2, CG), (1, TC * 2)])).then_inc(t_in[i], 16)

            load(0, 0, False)
            load(1, 1, False)
            with sp.Fori(1, NCG // 2) as j:
                for i in range(2):
                    load(2 * j + i, i, True)

        def gather(eng, copy, half, ready):
            def group(n, i, un):
                if not (isinstance(n, int) and n < 2):
                    eng.wait_ge(conv1, n - 1)
                rows = HALF + 1 - half
                for q in range(2):
                    at = (n - un * HG) * CQ + q * DQ
                    last = copy(ug[i][0:rows, half, q], u[un][0:rows, half, bass.ds(at, CQ)])
                last.then_inc(ready, 1)
            return group

        @block.gpsimd
        def _(pool):
            group = gather(pool, nc.gpsimd.tensor_copy, 1, u2_ready)
            group(0, 0, 0)
            group(1, 1, 0)
            with pool.Fori(1, HG // 2) as j:
                for i in range(2):
                    group(2 * j + i, i, 0)
            with pool.Fori(HG // 2, NCG // 2) as j:
                for i in range(2):
                    group(2 * j + i, i, 1)

        @block.tensor
        def _(pe):
            def group(n, i, guarded):
                pe.wait_ge(t_in[i], 16 * (n - i) + 32)
                pe.wait_ge(u_ready, n + 1)
                pe.wait_ge(u2_ready, n + 1)
                parts = ((0, 0), (1, 0), (0, 1))
                for bank, (done, used) in enumerate(((conv0, y0), (conv1, y1))):
                    if guarded:
                        pe.wait_ge(used, n - 1)
                    for c in range(2 * bank, 2 * bank + 2):
                        for a, (kk, uu) in enumerate(parts):
                            for q in range(2):
                                col = (c % 2) * TC
                                o = ps[q * B:(q + 1) * B, 2 * i + bank, col:col + TC]
                                nc.tensor.matmul(o, ug[i][:, 0, q, c, uu], t[i][:, q, c, ::-1, kk],
                                                 start=(a == 0), stop=False)
                        for a, (kk, uu) in enumerate(parts):
                            for q in range(2):
                                o = ps[q * B:(q + 1) * B, 2 * i + bank, col + HALF:col + TC]
                                last = nc.tensor.matmul(o, ug[i][0:HALF, 1, q, c, uu],
                                                        t[i][0:HALF, q, c, ::-1, kk][:, 0:HALF],
                                                        start=False, stop=(a == 2))
                    last.then_inc(done, 1)

            group(0, 0, False)
            group(1, 1, False)
            with pe.Fori(1, NCG // 2) as j:
                for i in range(2):
                    group(2 * j + i, i, True)

        def copy_out(eng, do, bank, done, ready, n, i, un):
            eng.wait_ge(ready, n + 1)
            at = (n - un * HG) * CQ + 2 * bank
            do(y[:, :, bass.ds(at, 2)].rearrange("p l c -> p c l"),
               ps[:, 2 * i + bank, 0:2 * TC].rearrange("p (c l) -> p c l", c=2)).then_inc(done, 1)

        @block.scalar
        def _(act):
            def scaled(o, a):
                return nc.scalar.mul(o, a, 1.0 / SCALE)

            def store(n):
                rows = mixed.rearrange("(b l) d -> b l d", l=SEQ)[:, 1:SEQ]
                act.wait_ge(y0, HG * (n + 1))
                act.wait_ge(y1, HG * (n + 1))
                for q in range(2):
                    at = n * DH + q * DQ
                    act.dma_start(rows[:, :, at:at + DQ], y[q * B:(q + 1) * B]).then_inc(y_out, 16)
                act.wait_ge(y_out, 32 * (n + 1))

            with act.Fori(0, HG // 2) as j:
                for i in range(2):
                    copy_out(act, scaled, 0, y0, conv0, 2 * j + i, i, 0)
            store(0)
            with act.Fori(HG // 2, NCG // 2) as j:
                for i in range(2):
                    copy_out(act, scaled, 0, y0, conv0, 2 * j + i, i, 1)
            store(1)

        @block.vector
        def _(dve):
            def scaled(o, a):
                return nc.vector.tensor_scalar(o, a, 1.0 / SCALE, None, ALU.mult)

            group = gather(dve, nc.vector.tensor_copy, 0, u_ready)
            group(0, 0, 0)
            group(1, 1, 0)
            with dve.Fori(1, HG // 2) as j:
                for i in range(2):
                    copy_out(dve, scaled, 1, y1, conv1, 2 * j + i - 2, i, 0)
                    group(2 * j + i, i, 0)
            for i in range(2):
                copy_out(dve, scaled, 1, y1, conv1, HG - 2 + i, i, 0)
                group(HG + i, i, 1)
            dve.wait_ge(y_out, 32)
            with dve.Fori(HG // 2 + 1, NCG // 2) as j:
                for i in range(2):
                    copy_out(dve, scaled, 1, y1, conv1, 2 * j + i - 2, i, 1)
                    group(2 * j + i, i, 1)
            for i in range(2):
                copy_out(dve, scaled, 1, y1, conv1, NCG - 2 + i, i, 1)


def feed_forward(nc, io, resid, mixed, out):
    with ExitStack() as ctx:
        def sb(name, shape, dt=F32):
            return ctx.enter_context(nc.sbuf_tensor(name, shape, dt))

        def sem(name):
            return ctx.enter_context(nc.semaphore(name))

        wa = [sb(f"wa_{n}", [128, 2, HID], F16) for n in ("hi", "lo")]
        wb = [sb(f"wb_{n}", [128, 2, HID], F16) for n in ("hi", "lo")]
        wd = [sb(f"wd_{n}", [128, NCH, D], F16) for n in ("hi", "lo")]
        wr = [sb(f"wr_{n}", [128, 2, E + 1], F16) for n in ("hi", "lo")]
        wrf = sb("wrf", [128, 2, E + 1])
        ident = sb("ident", [128, 128], F16)
        sel = sb("sel", [32, NRO, 128], F16)
        iota = sb("iota", [128, NT, E])
        sgb = sb("sgb", [128, NT, E + 1])
        mhalf = sb("mhalf2", [128, NT, 1])
        eps = sb("eps2", [128, NT, 1])
        WST = 1152
        stage = [sb(f"stage{i}", [128, WST]) for i in range(2)]
        pieces = []
        for x, (lo_hi, src) in enumerate(((wa, "w_a"), (wb, "w_b"))):
            for n in range(2 * HID // WST):
                pieces.append((lo_hi, src, n, "p k h -> p (k h)"))
        for n in range(NCH * D // WST):
            pieces.append((wd, "w_d", n, "p c d -> p (c d)"))

        hin = [sb(f"hin{i}", [128, NT, D]) for i in range(2)]
        yin = [sb(f"yin{i}", [128, NT, D]) for i in range(2)]
        h2 = [sb(f"h2_{i}", [128, NT, D]) for i in range(2)]
        ot = [sb(f"ot{i}", [128, NT, D]) for i in range(2)]
        st = sb("st2", [128, NT, 6])
        mv = sb("mv2", [128, NT, 2])
        ve = sb("ve2", [128, NT, 1])
        rs = sb("rs2", [128, NT, 1])
        xn = sb("xn", [128, NT, D])
        xs = sb("xs", [128, NT, XW], F16)
        xt = [sb(f"xt{i}", [128, 3, BT], F16) for i in range(2)]
        lg = sb("lg", [128, NT, E + 1])
        m8 = sb("m8", [128, NT, 8])
        ix = sb("ix", [128, NT, 8], U32)
        ixf = sb("ixf", [128, NT, 2])
        z = sb("z", [128, NT, 2])
        th = sb("th", [128, NT, 2])
        ga = sb("ga", [128, NT, 2])
        gb = sb("gb", [128, NT, 2])
        alpha = [sb(f"alpha{i}", [128, NT]) for i in range(2)]
        ea = sb("ea", [128, NT, E])
        eb = sb("eb", [128, NT, E])
        gs = sb("gs", [128, NT, 32], F16)
        gt = [sb(f"gt{i}", [32, BT], F16) for i in range(2)]
        sg = [sb(f"sg{i}", [128, BT]) for i in range(2)]
        hf = [sb(f"hf{i}", [128, BT]) for i in range(2)]
        hh = [sb(f"hh{i}", [128, BT], F16) for i in range(2)]
        hl = [sb(f"hl{i}", [128, BT], F16) for i in range(2)]

        psg = ctx.enter_context(nc.psum_tensor("psg", [128, 2, 512], F32))
        psu = ctx.enter_context(nc.psum_tensor("psu", [128, 2, 512], F32))
        psx = ctx.enter_context(nc.psum_tensor("psx", [128, 2, 512], F32))
        pso = ctx.enter_context(nc.psum_tensor("pso", [128, 2, 512], F32))
        px16 = [psx[:, i].bitcast(F16) for i in range(2)]

        names = ("const_in", "stage_in0", "stage_in1", "stage_hi", "stage_lo", "wrf_hi", "wr_ready", "memsets",
                 "rows_in0", "rows_in1", "h2_ready", "stats_ready", "mv_ready", "ve_ready", "rs_ready", "xn_ready",
                 "xhi_ready", "xlo_ready", "xt_ps", "xt_d", "xt_a", "lg_ps", "lg_ready", "route", "th_ready",
                 "gs_ready", "gt_ps", "gt_ready", "g_ps", "u_ps", "gb_ps", "sg_ready", "t_ready", "hf_ready",
                 "hh_ready", "hl_ready", "down", "shared_out", "out_ready", "stored0", "stored1")
        s = {name: sem("b_" + name) for name in names}
        block = ctx.enter_context(nc.Block())
        LOOPS = (NBLK - 3) // 2
        ROUTE = 13
        SHIFT = LAST_START

        def schedule(eng, body):
            body(0, 0, NT, NT)
            with eng.Fori(0, LOOPS) as j:
                for i in range(2):
                    body(2 * j + 1 + i, 1 - i, NT, NT)
            body(NBLK - 2, (NBLK - 2) % 2, NT, LAST_NT)
            body(NBLK - 1, (NBLK - 1) % 2, LAST_NT, 0)

        def rows(dram, b, nt):
            at = b * BT if nt == NT else SHIFT
            return dram[bass.ds(at, nt * 128)].rearrange("(t p) d -> p t d", p=128)

        def is_first(b):
            return isinstance(b, int) and b == 0

        @block.sync
        def _(sp):
            consts = ((wrf, "w_r"), (ident, "ident"), (sel, "sel"), (iota, "iota"), (sgb, "sgb"))
            for dst, src in consts:
                sp.dma_start(dst[:], io[src][:]).then_inc(s["const_in"], 16)

            def load(b, q, nt):
                sp.dma_start(hin[q][:, 0:nt], rows(resid, b, nt)).then_inc(s[f"rows_in{q}"], 16)
                sp.dma_start(yin[q][:, 0:nt], rows(mixed, b, nt)).then_inc(s[f"rows_in{q}"], 16)

            load(0, 0, NT)
            load(1, 1, NT)
            for n, (_, src, k, _) in enumerate(pieces):
                if n >= 2:
                    sp.wait_ge(s["stage_lo"], n - 1)
                sp.dma_start(stage[n % 2][:], io[src][:, k * WST:(k + 1) * WST]).then_inc(s[f"stage_in{n % 2}"], 16)

            def body(b, q, nt, nn):
                if not (isinstance(b, int) and b >= NBLK - 3) :
                    sp.wait_ge(s["h2_ready"], b + 1)
                    load(b + 2, q, NT)

            body(0, 0, NT, NT)
            with sp.Fori(0, LOOPS - 1) as j:
                for i in range(2):
                    body(2 * j + 1 + i, 1 - i, NT, NT)
            body_last = ((NBLK - 4, NT), (NBLK - 3, LAST_NT))
            for b, nt in body_last:
                sp.wait_ge(s["h2_ready"], b + 1)
                load(b + 2, b % 2, nt)

        def chunk_sem(b, m):
            return NCH * b + m

        @block.tensor
        def _(pe):
            def transposes(b, q, nt):
                pe.wait_ge(s["xlo_ready"], b + 1)
                for c in range(3):
                    for t in range(nt):
                        o = px16[c // 2][:, (c % 2) * BT + t * 128:(c % 2) * BT + (t + 1) * 128]
                        last = nc.tensor.transpose(o, xs[:, t, c * 128:(c + 1) * 128], ident[:])
                    if c:
                        last.then_inc(s["xt_ps"], 1)

            def router(b, q, nt):
                pe.wait_ge(s["xt_d"], b + 1)
                pe.wait_ge(s["xt_a"], b + 1)
                for t in range(nt):
                    o = psx[:, 1, 256 + 16 * t:256 + 16 * t + E + 1]
                    ts = slice(t * 128, (t + 1) * 128)
                    prods = ((0, wr[0][:, 0]), (0, wr[1][:, 0]), (2, wr[0][:, 0]), (1, wr[0][:, 1]), (1, wr[1][:, 1]))
                    for a, (c, r) in enumerate(prods):
                        last = nc.tensor.matmul(o, xt[q][:, c, ts], r, start=(a == 0), stop=(a == 4))
                last.then_inc(s["lg_ps"], 1)

            def gates_turn(b, q, nt):
                pe.wait_ge(s["gs_ready"], b + 1)
                for t in range(nt):
                    last = nc.tensor.transpose(px16[1][0:32, t * 128:(t + 1) * 128], gs[:, t, :], ident[:])
                last.then_inc(s["gt_ps"], 1)

            def up(b, q, nt, nn, m):
                n = nt * 128
                if m >= 2 or not is_first(b):
                    pe.wait_ge(s["hf_ready"], chunk_sem(b, m) - 1)
                for k, (ps, done) in enumerate(((psg, "g_ps"), (psu, "u_ps"))):
                    cols = slice(m * 128, (m + 1) * 128)
                    prods = ((wa[0], 0), (wa[1], 0), (wa[0], 2), (wb[0], 1), (wb[1], 1))
                    for a, (wt, c) in enumerate(prods):
                        last = nc.tensor.matmul(ps[:, m % 2, 0:n], wt[:, k, cols], xt[q][:, c, 0:n],
                                                start=(a == 0), stop=(a == 4))
                    last.then_inc(s[done], 1)
                if m >= NSH:
                    if m == NSH:
                        pe.wait_ge(s["gt_ready"], b + (2 if nn else 1))
                    nc.tensor.matmul(psx[:, m % 2, 0:n], sel[:, m - NSH], gt[q][:, 0:n], start=True,
                                     stop=True).then_inc(s["gb_ps"], 1)

            def down(b, nt, m):
                pe.wait_ge(s["hl_ready"], chunk_sem(b, m) + 1)
                if m == 0 and not is_first(b):
                    pe.wait_ge(s["out_ready"], b)
                if m == NSH:
                    pe.wait_ge(s["shared_out"], b + 1)
                for t in range(nt):
                    o = pso[:, t // 2, (t % 2) * D:(t % 2 + 1) * D]
                    ts = slice(t * 128, (t + 1) * 128)
                    prods = ((hh, 0), (hh, 1), (hl, 0))
                    for a, (hx, k) in enumerate(prods):
                        last = nc.tensor.matmul(o, hx[m % 2][:, ts], wd[k][:, m],
                                                start=(a == 0 and m in (0, NSH) and t % 2 == 0),
                                                stop=(a == 2 and m in (NSH - 1, NCH - 1)), skip_group_check=True)
                last.then_inc(s["down"], 1)

            pe.wait_ge(s["const_in"], 80)
            pe.wait_ge(s["wr_ready"], 1)
            pe.wait_ge(s["memsets"], 5)
            transposes(0, 0, NT)
            router(0, 0, NT)
            gates_turn(0, 0, NT)
            pe.wait_ge(s["stage_lo"], len(pieces))

            def body(b, q, nt, nn):
                for m in range(NCH):
                    up(b, q, nt, nn, m)
                    if m >= 2:
                        down(b, nt, m - 2)
                    elif not is_first(b):
                        down(b - 1, NT, NCH - 2 + m)
                    if nn and m == 2:
                        transposes(b + 1, 1 - q, nn)
                    if nn and m == 3:
                        router(b + 1, 1 - q, nn)
                    if nn and m == 5:
                        gates_turn(b + 1, 1 - q, nn)

            schedule(pe, body)
            for m in (NCH - 2, NCH - 1):
                down(NBLK - 1, LAST_NT, m)

        @block.scalar
        def _(act):
            act.wait_ge(s["const_in"], 80)
            nc.scalar.mul(wrf[:], wrf[:], SCALE).then_inc(s["wrf_hi"], 1)
            act.wait_ge(s["wrf_hi"], 1)
            nc.scalar.copy(wr[0][:], wrf[:]).then_inc(s["wrf_hi"], 1)

            def x_high(b, nt):
                act.wait_ge(s["xn_ready"], b + 1)
                if not is_first(b):
                    act.wait_ge(s["xt_ps"], 2 * b)
                nc.scalar.copy(xs[:, 0:nt, 0:D], xn[:, 0:nt]).then_inc(s["xhi_ready"], 1)

            def x_out(b, q, nt):
                act.wait_ge(s["xt_ps"], 2 * b + 2)
                nc.scalar.copy(xt[q][:, 2, 0:nt * 128], px16[1][:, 0:nt * 128]).then_inc(s["xt_a"], 1)

            def tanh(b, nt):
                act.wait_ge(s["route"], ROUTE * b + 3)
                nc.scalar.activation(th[:, 0:nt], z[:, 0:nt], ACT.Tanh, scale=0.5).then_inc(s["th_ready"], 1)

            def gates_out(b, q, nt):
                act.wait_ge(s["gt_ps"], b + 1)
                nc.scalar.copy(gt[q][:, 0:nt * 128], px16[1][0:32, 0:nt * 128]).then_inc(s["gt_ready"], 1)

            def silu(b, nt, m):
                n = nt * 128
                act.wait_ge(s["g_ps"], chunk_sem(b, m) + 1)
                if m >= 2 or not is_first(b):
                    act.wait_ge(s["hf_ready"], chunk_sem(b, m) - 1)
                nc.scalar.activation(sg[m % 2][:, 0:n], psg[:, m % 2, 0:n], ACT.Silu,
                                     scale=1.0 / SCALE).then_inc(s["sg_ready"], 1)

            def high(b, nt, m, first=False):
                n = nt * 128
                act.wait_ge(s["hf_ready"], chunk_sem(b, m) + 1)
                if not first:
                    act.wait_ge(s["down"], chunk_sem(b, m) - 1)
                nc.scalar.copy(hh[m % 2][:, 0:n], hf[m % 2][:, 0:n]).then_inc(s["hh_ready"], 1)

            def store(b, q, nt):
                act.wait_ge(s["out_ready"], b + 1)
                if nt == LAST_NT:
                    for i in range(2):
                        act.wait_ge(s[f"stored{i}"], 8 * b + 16)
                act.dma_start(rows(out, b, nt), ot[q][:, 0:nt]).then_inc(s[f"stored{q}"], 16)

            x_high(0, NT)
            for n, (dst, _, k, fl) in enumerate(pieces):
                act.wait_ge(s[f"stage_in{n % 2}"], 16 * (n // 2 + 1))
                view = dst[0][:].rearrange(fl)[:, k * WST:(k + 1) * WST]
                nc.scalar.mul(view, stage[n % 2][:], SCALE).then_inc(s["stage_hi"], 1)
            x_out(0, 0, NT)
            tanh(0, NT)
            gates_out(0, 0, NT)

            def body(b, q, nt, nn):
                for m in range(NCH):
                    silu(b, nt, m)
                    if m >= 1:
                        high(b, nt, m - 1, first=is_first(b) and m - 1 < 2)
                    elif not is_first(b):
                        high(b - 1, NT, NCH - 1)
                    if m == 2 and not is_first(b):
                        store(b - 1, 1 - q, NT)
                    if nn and m == 1:
                        x_high(b + 1, nn)
                    if nn and m == 3:
                        x_out(b + 1, 1 - q, nn)
                    if nn and m == 4:
                        tanh(b + 1, nn)
                    if nn and m == 5:
                        gates_out(b + 1, 1 - q, nn)

            schedule(act, body)
            high(NBLK - 1, LAST_NT, NCH - 1)
            store(NBLK - 1, (NBLK - 1) % 2, LAST_NT)
            act.wait_ge(s[f"stored{(NBLK - 1) % 2}"], 8 * (NBLK + 1) + 16)

        @block.gpsimd
        def _(pool):
            nc.gpsimd.memset(mhalf[:], -0.5).then_inc(s["memsets"], 1)
            nc.gpsimd.memset(eps[:], EPS).then_inc(s["memsets"], 1)
            nc.gpsimd.memset(gs[:], 0.0).then_inc(s["memsets"], 1)
            nc.gpsimd.memset(hl[0][:], 0.0).then_inc(s["memsets"], 1)
            nc.gpsimd.memset(hl[1][:], 0.0).then_inc(s["memsets"], 1)
            pool.wait_ge(s["memsets"], 5)

            def rstd(b, nt):
                pool.wait_ge(s["mv_ready"], b + 1)
                nc.gpsimd.tensor_tensor(ve[:, 0:nt], mv[:, 0:nt, 1:2], eps[:, 0:nt], ALU.add).then_inc(s["ve_ready"], 1)
                pool.wait_ge(s["ve_ready"], b + 1)
                nc.gpsimd.tensor_tensor(rs[:, 0:nt], ve[:, 0:nt], mhalf[:, 0:nt], ALU.pow).then_inc(s["rs_ready"], 1)

            def x_low(b, nt):
                pool.wait_ge(s["xhi_ready"], b + 1)
                nc.gpsimd.tensor_tensor(xs[:, 0:nt, D:D + 64], xn[:, 0:nt, 128:D], xs[:, 0:nt, 128:D], ALU.subtract)
                nc.gpsimd.tensor_tensor(xs[:, 0:nt, D + 64:XW], xn[:, 0:nt, 0:128], xs[:, 0:nt, 0:128],
                                        ALU.subtract).then_inc(s["xlo_ready"], 1)

            def low(b, nt, m, first=False):
                n = nt * 128
                pool.wait_ge(s["hh_ready"], chunk_sem(b, m) + 1)
                nc.gpsimd.tensor_tensor(hl[m % 2][:, 0:n], hf[m % 2][:, 0:n], hh[m % 2][:, 0:n],
                                        ALU.subtract).then_inc(s["hl_ready"], 1)

            rstd(0, NT)
            x_low(0, NT)

            def body(b, q, nt, nn):
                for m in range(NCH):
                    if nn and m == 0:
                        rstd(b + 1, nn)
                    if m >= 1:
                        low(b, nt, m - 1)
                    elif not is_first(b):
                        low(b - 1, NT, NCH - 1)
                    if nn and m == 1:
                        x_low(b + 1, nn)

            schedule(pool, body)
            low(NBLK - 1, LAST_NT, NCH - 1)

        @block.vector
        def _(dve):
            dve.wait_ge(s["memsets"], 5)
            dve.wait_ge(s["const_in"], 80)
            dve.wait_ge(s["wrf_hi"], 2)
            nc.vector.tensor_tensor(wr[1][:], wrf[:], wr[0][:], ALU.subtract).then_inc(s["wr_ready"], 1)

            def add(b, q, nt):
                dve.wait_ge(s[f"rows_in{q}"], 16 * (b - q) + 32)
                nc.vector.tensor_tensor(h2[q][:, 0:nt], hin[q][:, 0:nt], yin[q][:, 0:nt],
                                        ALU.add).then_inc(s["h2_ready"], 1)
                dve.wait_ge(s["h2_ready"], b + 1)
                for t in range(nt):
                    last = nc.vector.bn_stats(st[:, t], h2[q][:, t])
                last.then_inc(s["stats_ready"], 1)
                dve.wait_ge(s["memsets"], 5)
                dve.wait_ge(s["stats_ready"], b + 1)
                for t in range(nt):
                    last = nc.vector.bn_aggr(mv[:, t], st[:, t])
                last.then_inc(s["mv_ready"], 1)

            def normal(b, q, nt):
                dve.wait_ge(s["rs_ready"], b + 1)
                for t in range(nt):
                    last = nc.vector.tensor_scalar(xn[:, t], h2[q][:, t], mv[:, t, 0:1], rs[:, t], ALU.subtract,
                                                   ALU.mult)
                last.then_inc(s["xn_ready"], 1)

            def x_out(b, q, nt):
                dve.wait_ge(s["xt_ps"], 2 * b + 1)
                n = nt * 128
                nc.vector.tensor_copy(xt[q][:, 0:2, 0:n],
                                      px16[0][:, 0:2 * BT].rearrange("p (c n) -> p c n", c=2)[:, :, 0:n]
                                      ).then_inc(s["xt_d"], 1)

            def logits(b, q, nt):
                k = [0]

                def step(ins):
                    k[0] += 1
                    ins.then_inc(s["route"], 1)
                    dve.wait_ge(s["route"], ROUTE * b + k[0])

                dve.wait_ge(s["lg_ps"], b + 1)
                src = psx[:, 1, 256:256 + 16 * nt].rearrange("p (t e) -> p t e", e=16)[:, :, 0:E + 1]
                step(nc.vector.scalar_tensor_tensor(out=lg[:, 0:nt], in0=src, scalar=1.0 / SCALE, in1=sgb[:, 0:nt],
                                                    op0=ALU.mult, op1=ALU.add))
                nc.vector.tensor_copy(z[:, 0:nt, 1:2], lg[:, 0:nt, E:E + 1])
                for t in range(nt):
                    last = nc.vector.max(m8[:, t], lg[:, t, 0:E])
                step(last)
                k[0] += 1
                nc.vector.tensor_tensor(z[:, 0:nt, 0:1], m8[:, 0:nt, 0:1], m8[:, 0:nt, 1:2],
                                        ALU.subtract).then_inc(s["route"], 1)
                for t in range(nt):
                    last = nc.vector.max_index(ix[:, t], m8[:, t], lg[:, t, 0:E])
                step(last)
                step(nc.vector.tensor_copy(ixf[:, 0:nt], ix[:, 0:nt, 0:2]))
                shape = [128, nt, E]
                nc.vector.tensor_tensor(ea[:, 0:nt], iota[:, 0:nt], ixf[:, 0:nt, 0:1].to_broadcast(shape), ALU.is_equal)
                step(nc.vector.tensor_tensor(eb[:, 0:nt], iota[:, 0:nt], ixf[:, 0:nt, 1:2].to_broadcast(shape),
                                             ALU.is_equal))
                dve.wait_ge(s["th_ready"], b + 1)
                nc.vector.tensor_scalar(ga[:, 0:nt], th[:, 0:nt], 0.5, 0.5, ALU.mult, ALU.add)
                step(nc.vector.tensor_scalar(gb[:, 0:nt], th[:, 0:nt], -0.5, 0.5, ALU.mult, ALU.add))
                nc.vector.tensor_scalar(alpha[q][:, 0:nt], ga[:, 0:nt, 1], 1.0 / SCALE, None, ALU.mult)
                nc.vector.tensor_tensor(ea[:, 0:nt], ea[:, 0:nt], ga[:, 0:nt, 0:1].to_broadcast(shape), ALU.mult)
                step(nc.vector.tensor_tensor(eb[:, 0:nt], eb[:, 0:nt], gb[:, 0:nt, 0:1].to_broadcast(shape), ALU.mult))
                step(nc.vector.tensor_tensor(ea[:, 0:nt], ea[:, 0:nt], eb[:, 0:nt], ALU.add))
                step(nc.vector.tensor_tensor(ea[:, 0:nt], ea[:, 0:nt], gb[:, 0:nt, 1:2].to_broadcast(shape), ALU.mult))
                step(nc.vector.tensor_copy(gs[:, 0:nt, 0:E], ea[:, 0:nt]))
                step(nc.vector.tensor_tensor(eb[:, 0:nt], ea[:, 0:nt], gs[:, 0:nt, 0:E], ALU.subtract))
                step(nc.vector.tensor_copy(gs[:, 0:nt, 16:16 + E], eb[:, 0:nt]))
                assert k[0] == ROUTE
                nc.vector.tensor_copy(ixf[:, 0:nt], ixf[:, 0:nt]).then_inc(s["gs_ready"], 1)

            def hidden(b, nt, m):
                n = nt * 128
                i = m % 2
                dve.wait_ge(s["sg_ready"], chunk_sem(b, m) + 1)
                dve.wait_ge(s["u_ps"], chunk_sem(b, m) + 1)
                if m >= 2 or not is_first(b):
                    dve.wait_ge(s["hl_ready"], chunk_sem(b, m) - 1)
                ins = nc.vector.scalar_tensor_tensor(out=hf[i][:, 0:n], in0=psu[:, i, 0:n], scalar=1.0 / SCALE,
                                                     in1=sg[i][:, 0:n], op0=ALU.mult, op1=ALU.mult)
                if m < NSH:
                    ins.then_inc(s["hf_ready"], 1)
                    return
                ins.then_inc(s["t_ready"], 1)
                dve.wait_ge(s["t_ready"], NRO * b + m - NSH + 1)
                dve.wait_ge(s["gb_ps"], NRO * b + m - NSH + 1)
                nc.vector.tensor_tensor(hf[i][:, 0:n], psx[:, i, 0:n], hf[i][:, 0:n],
                                        ALU.mult).then_inc(s["hf_ready"], 1)

            def shared_out(b, q, nt):
                dve.wait_ge(s["down"], chunk_sem(b, NSH))
                if not is_first(b) and not (isinstance(b, int) and b < 2):
                    dve.wait_ge(s[f"stored{q}"], 8 * (b - q) + 16)
                for t in range(nt):
                    last = nc.vector.scalar_tensor_tensor(
                        out=ot[q][:, t], in0=pso[:, t // 2, (t % 2) * D:(t % 2 + 1) * D],
                        scalar=alpha[q][:, t:t + 1], in1=h2[q][:, t], op0=ALU.mult, op1=ALU.add)
                last.then_inc(s["shared_out"], 1)

            def routed_out(b, q, nt):
                dve.wait_ge(s["down"], chunk_sem(b, NCH))
                dve.wait_ge(s["shared_out"], b + 1)
                for t in range(0, nt, 2):
                    c = min(2, nt - t)
                    o = ot[q][:, t:t + c].rearrange("p t d -> p (t d)")
                    last = nc.vector.scalar_tensor_tensor(out=o, in0=pso[:, t // 2, 0:c * D], scalar=1.0 / SCALE,
                                                          in1=o, op0=ALU.mult, op1=ALU.add)
                last.then_inc(s["out_ready"], 1)

            for i in range(2):
                dve.sem_inc(s[f"stored{i}"], 16)
            add(0, 0, NT)
            normal(0, 0, NT)
            for n, (dst, _, k, fl) in enumerate(pieces):
                dve.wait_ge(s["stage_hi"], n + 1)
                hi, lo = (x[:].rearrange(fl)[:, k * WST:(k + 1) * WST] for x in dst)
                nc.vector.scalar_tensor_tensor(out=lo, in0=stage[n % 2][:], scalar=SCALE, in1=hi, op0=ALU.mult,
                                               op1=ALU.subtract).then_inc(s["stage_lo"], 1)
            x_out(0, 0, NT)
            logits(0, 0, NT)

            def body(b, q, nt, nn):
                for m in range(NCH):
                    hidden(b, nt, m)
                    if nn and m == 0:
                        add(b + 1, 1 - q, nn)
                        normal(b + 1, 1 - q, nn)
                    if m == 1 and not is_first(b):
                        routed_out(b - 1, 1 - q, NT)
                    if nn and m == 2:
                        x_out(b + 1, 1 - q, nn)
                    if nn and m == 3:
                        logits(b + 1, 1 - q, nn)
                    if m == NSH + 1:
                        shared_out(b, q, nt)

            schedule(dve, body)
            routed_out(NBLK - 1, (NBLK - 1) % 2, LAST_NT)


def build(nc, io, out):
    taps = nc.dram_tensor("taps", (D, RW, 2), F16, kind="Internal").ap()
    resid = nc.dram_tensor("resid", (NTOK, D), F32, kind="Internal").ap()
    mixed = nc.dram_tensor("mixed", (NTOK, D), F32, kind="Internal").ap()
    out_rows = out.rearrange("b l d -> (b l) d")
    with ExitStack() as ctx:
        u = [ctx.enter_context(nc.sbuf_tensor(f"u{i}", [HALF + 1, 2, DH, 2, B], F16)) for i in range(2)]
        with ExitStack() as emb:
            w = {"hi": emb.enter_context(nc.sbuf_tensor("w_hi", [ROWS, C, D], F16)),
                 "lo": emb.enter_context(nc.sbuf_tensor("w_lo", [ROWS, C, D], F16)),
                 "x": emb.enter_context(nc.sbuf_tensor("w_x", [NX, D], F16)),
                 "signs": emb.enter_context(nc.sbuf_tensor("signs", [NX, 2], F32))}
            load_signs(nc, io, w)
            prepare(nc, io, u, w, (taps, resid, mixed))
            embed(nc, io, u, w, resid)
        mix(nc, u, taps, mixed)
    feed_forward(nc, io, resid, mixed, out_rows)


def load_signs(nc, io, w):
    with nc.semaphore("signs_in") as signs_in, nc.Block() as block:
        @block.sync
        def _(sp):
            sp.dma_start(w["signs"][:], io["signs"][:]).then_inc(signs_in, 16)
            sp.wait_ge(signs_in, 16)


def constants():
    fa, fx = dft_constants()
    signs = np.zeros((NX, 2), np.float32)
    signs[6:12, 0] = -1.0
    signs[12:18, 1] = -1.0
    sel = np.zeros((32, NRO, 128), np.float16)
    for m in range(NRO):
        for r in range(128):
            e = (m * 128 + r) // HE
            sel[e, m, r] = sel[16 + e, m, r] = 1.0
    iota = np.broadcast_to(np.arange(E, dtype=np.float32), (128, NT, E))
    return {"fa": fa, "fx": fx, "signs": signs, "sel": sel, "iota": np.ascontiguousarray(iota),
            "ident": np.eye(128, dtype=np.float16)}


def layout(inputs):
    g = {k.replace("L0_", ""): np.asarray(v) for k, v in inputs.items()}
    first, second, _, rest = pixel_fold()
    x = g["x"].reshape(B, C, SIDE, P, SIDE, P).transpose(1, 3, 5, 0, 2, 4).reshape(C, P * P, NG, GT)

    def pick(pix):
        return x[:, [r * P + s for r, s in pix]]

    a = {"xa": pick(first).transpose(2, 1, 0, 3), "xb": pick(second).transpose(2, 1, 0, 3)}
    rest = pick(rest).transpose(2, 0, 1, 3).reshape(NG, 2 * C, GT)
    a["xe"] = np.tile(rest, (1, 3, 1))
    a["pw"] = g["tok_proj_w"].T.reshape(C, 2, FCH, D).transpose(2, 1, 0, 3)
    wh = np.repeat(g["tok_freq_weight_h"], KW).reshape(2, FCH)
    ww = np.tile(g["tok_freq_weight_w"], KH).reshape(2, FCH)
    a["freq"] = np.stack([wh, ww]).transpose(2, 0, 1)
    pos = g["tok_position_embeddings"][0]
    bias = np.broadcast_to(g["tok_proj_b"], (HALF, 2, D))
    a["pos"] = np.stack([bias, pos[1:].reshape(2, HALF, D).transpose(1, 0, 2)])
    a["cls"] = np.broadcast_to(np.stack([g["tok_cls_token"][0, 0], pos[0]]), (3, 2, D))

    def states(m):
        m = m.reshape(2, 2, NCG // 2, CG // 2, NST).transpose(0, 4, 2, 1, 3)
        return m.reshape(128, DH)

    delta = np.broadcast_to(g["attn_delta"][:, None], (D, NST))
    a["ssm"] = np.stack([states(m) for m in (g["attn_A_re"], g["attn_A_im"], g["attn_B_mat"], g["attn_C_mat"], delta)], 1)
    gate = np.concatenate([g["ffn_ws_gate"], g["ffn_w_gate"].transpose(1, 0, 2).reshape(D, E * HE)], 1)
    upw = np.concatenate([g["ffn_ws_up"], g["ffn_w_up"].transpose(1, 0, 2).reshape(D, E * HE)], 1)
    both = np.concatenate([gate, upw], 1)
    a["w_a"] = both[0:128]
    a["w_b"] = np.concatenate([both[128:D], both[128:D]], 0)
    dn = np.concatenate([g["ffn_ws_down"], g["ffn_w_down"].reshape(E * HE, D)], 0)
    a["w_d"] = dn.reshape(NCH, 128, D).transpose(1, 0, 2).reshape(128, NCH * D)
    r = np.concatenate([g["ffn_router_w"], g["ffn_sg_w"]], 1)
    a["w_r"] = np.stack([r[0:128], np.concatenate([r[128:D], r[128:D]], 0)], 1)
    sgb = np.zeros((128, NT, E + 1), np.float32)
    sgb[:, :, E] = g["ffn_sg_b"][0]
    a["sgb"] = sgb
    a.update(constants())
    return {k: np.ascontiguousarray(v) for k, v in a.items()}


def kernel(**inputs):
    import concourse.bacc as _bacc
    from concourse import mybir as _mybir
    from concourse.bass_utils import run_bass_kernel_spmd as _run

    nc = _bacc.Bacc("TRN2", target_bir_lowering=False, num_devices=1)
    arrays, io = {}, {}
    for name, a in layout(inputs).items():
        arrays[f"in_{name}_dram"] = a
        io[name] = nc.dram_tensor(f"in_{name}_dram", a.shape, _mybir.dt.from_np(a.dtype), kind="ExternalInput").ap()
    out = nc.dram_tensor("out_0_dram", (B, SEQ, D), _mybir.dt.float32, kind="ExternalOutput").ap()
    build(nc, io, out)
    r = _run(nc, [arrays], core_ids=[0])
    return r.results[0]["out_0_dram"]
```

```python
from contextlib import ExitStack

import numpy as np
import concourse.bass as bass
from concourse import mybir

F32 = mybir.dt.float32
F16 = mybir.dt.float16
U32 = mybir.dt.uint32
ALU = mybir.AluOpType
ACT = mybir.ActivationFunctionType

B, C, IMG, P = 64, 3, 224, 16
SIDE = IMG // P
NPATCH = SIDE * SIDE
HALF = NPATCH // 2
SEQ = NPATCH + 1
D = 192
DH = D // 2
KH, KW = P, P // 2 + 1
NFREQ = KH * KW
FCH = NFREQ // 2
NST = 64
E, HE, HS = 8, 192, 768
EPS = 1e-5
SCALE = 16.0

GI = 4
NG = B // GI
GT = GI * NPATCH
ROWS = 128
NX = 18

KA, KB = 15, 14
KL = KA * KB
CG = 8
NCG = D // CG
TC = NPATCH
DQ = DH // 2
SKIP = KL - SEQ
RW = SKIP + 1 + HALF + TC
AREA = max(3 * 2 * KA * DH, 4 * C * GT, NPATCH * DQ)

NTOK = B * SEQ
BT, NT = 512, 4
LAST_NT = 3
NBLK = NTOK // BT + 1
LAST_START = NTOK - LAST_NT * 128
FIRST_IMAGES = -(-2 * BT // SEQ)
NSH = HS // 128
XW = 2 * D
RX = XW + 8
W_SHARED = 4 * HS + NSH * D
W_EXPERT = 4 * HE + 2 * D
W_COLS = W_SHARED + E * W_EXPERT
UNIT = BT
CAP = NTOK + UNIT
FILL = E * CAP
NFILL = 3
XROWS = FILL + NFILL * UNIT
OUT_ROWS = NTOK + UNIT
NU = 60
MAX_UNITS = 2 * NTOK // UNIT + E
MIN_UNITS = -(-2 * NTOK // UNIT)


def pixel_fold():
    pairs, selfs = [], []
    for r in range(P):
        for s in range(P):
            q = ((-r) % P, (-s) % P)
            if q == (r, s):
                selfs.append((r, s))
            elif (r, s) < q:
                pairs.append(((r, s), q))
    first = [p for p, _ in pairs] + selfs[:2]
    second = [q for _, q in pairs] + selfs[:2]
    return first, second, len(pairs), selfs[2:]


def dft_constants():
    first, _, npairs, rest = pixel_fold()
    kh, kw = np.meshgrid(np.arange(KH), np.arange(KW), indexing="ij")
    kh, kw = kh.reshape(-1), kw.reshape(-1)

    def col(p):
        return np.cos(2 * np.pi * ((kh * p[0] + kw * p[1]) % P) / P) / P

    fa = np.stack([col(p) * (1.0 if n < npairs else 0.5) for n, p in enumerate(first)], 1)
    fx = np.zeros((NFREQ, C, NX))
    for c in range(C):
        for rep in range(3):
            for k, p in enumerate(rest):
                fx[:, c, rep * 6 + c * 2 + k] = col(p)
    fa = fa.reshape(2, FCH, ROWS).transpose(1, 0, 2)
    fx = fx.reshape(2, FCH, C, NX).transpose(1, 0, 2, 3)
    return np.ascontiguousarray(fa, np.float32), np.ascontiguousarray(fx, np.float32)


def pixel_tiles(area):
    return ([area[:, (2 * i + n) * C * GT:(2 * i + n + 1) * C * GT].rearrange("p (c t) -> p c t", c=C)
             for i in range(2)] for n in range(2))


def load_pixels(sp, io, w, area, g, i):
    xa, xb = pixel_tiles(area)
    for dst, src in ((xa[i], "xa"), (xb[i], "xb")):
        sp.dma_start(dst, io[src][bass.ds(g, 1)].rearrange("g p c t -> (g p) c t")).then_inc(w["x_in"][i], 16)
    sp.dma_start(w["xe"][i][:], io["xe"][bass.ds(g, 1)].rearrange("g p t -> (g p) t")).then_inc(w["x_in"][i], 16)


def prepare(nc, io, u, w, area, scratch):
    taps, resid, mixed = scratch
    with ExitStack() as ctx:
        def sb(name, shape, dt=F32):
            return ctx.enter_context(nc.sbuf_tensor(name, shape, dt))

        def sem(name):
            return ctx.enter_context(nc.semaphore(name))

        fa = sb("fa", [FCH, 2, ROWS])
        fx = sb("fx", [FCH, 2, C, NX])
        pw = sb("pw", [FCH, 2, C, D])
        freq = sb("freq", [FCH, 2, 2])
        fw = sb("fw", [FCH, 2])
        pws = sb("pws", [FCH, 2, C, D])
        wf = sb("wf", [ROWS, C, D])
        wxf = sb("wxf", [NX, D])
        wxh = sb("wxh", [NX, D], F16)
        ssm = sb("ssm", [128, 5, DH])
        v = sb("v", [128, 2, DH])
        p = sb("p", [128, 2, DH])
        e1 = sb("e1", [128, 2, DH])
        cf = sb("cf", [128, 2, DH])
        q = sb("q", [128, 4, DH])
        sr, si, tq = (area[:, i * 2 * KA * DH:(i + 1) * 2 * KA * DH].rearrange("p (k a d) -> p k a d", k=2, a=KA)
                      for i in range(3))
        tp = sb("tp", [128, 2, KA, DH])
        zq = sb("zq", [128, 2, KB, DH])
        zp = sb("zp", [128, 2, DH, KA])
        kf = zq[0:CG * KA].rearrange("p k b d -> p (k b d)").rearrange("p (g c) -> p g c", g=NCG)
        ks = zp[0:CG * KA].rearrange("p k d a -> p (k d a)")[:, 0:NCG * CG * KB].bitcast(F16).rearrange(
            "p (g c k) -> p g c k", g=NCG, k=2)
        zero = sb("zero", [DH, 2 * (RW - KL)], F16)
        cl = sb("cl", [3, 2, D])
        hc = sb("hc", [3, D])
        cst = sb("cst", [3, 6])
        cmv = sb("cmv", [3, 2])
        cve = sb("cve", [3, 1])
        crs = sb("crs", [3, 1])
        chalf = sb("chalf", [3, 1])
        uc = sb("uc", [3, D])
        ucs = sb("ucs", [3, D, 2], F16)
        k0 = sb("k0", [1, D, 2], F16)
        k0f = sb("k0f", [1, D])
        yc = sb("yc", [1, D])
        psw = ctx.enter_context(nc.psum_tensor("psw", [128, 2, 512], F32))
        psk = ctx.enter_context(nc.psum_tensor("psk", [128, 6, 512], F32))

        loaded_w, loaded_a, loaded_c = sem("loaded_w"), sem("loaded_a"), sem("loaded_c")
        d = sem("vector_done")
        pws_ready, wps_ready, powers_ready, taps_ready = (
            sem("pws_ready"), sem("wps_ready"), sem("powers_ready"), sem("taps_ready"))
        zero_ready, split_ready, hc_ready, cmv_ready = (
            sem("zero_ready"), sem("split_ready"), sem("hc_ready"), sem("cmv_ready"))
        g, crs_ready, ucs_ready, rep_done = sem("gp"), sem("crs_ready"), sem("ucs_ready"), sem("rep_done")
        taps_out, k0_in, yc_ready, out_done = sem("taps_out"), sem("k0_in"), sem("yc_ready"), sem("out_done")

        block = ctx.enter_context(nc.Block())

        @block.sync
        def _(sp):
            for dst, src in ((fa, "fa"), (fx, "fx"), (pw, "pw"), (freq, "freq")):
                sp.dma_start(dst[:], io[src][:]).then_inc(loaded_w, 16)
            sp.dma_start(ssm[:], io["ssm"][:]).then_inc(loaded_a, 16)
            sp.dma_start(cl[:], io["cls"][:]).then_inc(loaded_c, 16)
            sp.wait_ge(powers_ready, 1)
            for i in range(2):
                load_pixels(sp, io, w, area, i, i)
            sp.wait_ge(zero_ready, 1)
            for n in range(2):
                rows = taps[n * DH:(n + 1) * DH]
                sp.dma_start(rows[:, KL:RW, :].rearrange("r c k -> r (c k)"), zero[:]).then_inc(taps_out, 16)
            sp.wait_ge(split_ready, 1)
            for i in range(CG):
                dst = bass.AP(taps.tensor, i * RW * 2,
                              [(2 * KB, KA), (CG * RW * 2, NCG), (1, 2 * KB)])
                src = ks[i * KA:(i + 1) * KA, :, i * KB:(i + 1) * KB, :].rearrange("a g b k -> a g (b k)")
                sp.dma_start(dst, src).then_inc(taps_out, 16)
            sp.wait_ge(taps_out, 16 * (2 + CG))
            with nc.allow_non_contiguous_dma(reason="one tap of each channel"):
                for n in range(2):
                    for q in range(2):
                        rows = taps[n * DH:(n + 1) * DH, KL - 1, :].rearrange("(g q c) k -> q g c k", q=2, c=CG // 2)
                        dst = k0[:, n * DH + q * DQ:n * DH + (q + 1) * DQ, :]
                        sp.dma_start(dst.rearrange("p (g c) k -> p g c k", c=CG // 2),
                                     rows[q:q + 1]).then_inc(k0_in, 16)
            sp.wait_ge(hc_ready, 1)
            sp.dma_start(resid.rearrange("(b l) d -> l b d", l=SEQ)[0:1],
                         hc[0:1, :].unsqueeze(1).to_broadcast([1, B, D])).then_inc(out_done, 16)
            sp.wait_ge(yc_ready, 1)
            for c in range(4):
                sp.dma_start(mixed[c].rearrange("(b l) d -> l b d", l=SEQ)[0:1],
                             yc[0:1, c * DQ:(c + 1) * DQ].unsqueeze(1).to_broadcast([1, B, DQ])
                             ).then_inc(out_done, 16)
            sp.wait_ge(out_done, 16 * 5)

        @block.gpsimd
        def _(pool):
            nc.gpsimd.memset(zero[:], 0.0).then_inc(zero_ready, 1)
            nc.gpsimd.memset(chalf[:], -0.5).then_inc(g, 1)
            pool.wait_ge(cmv_ready, 1)
            nc.gpsimd.tensor_scalar(cve[:], cmv[:, 1:2], EPS, None, ALU.add).then_inc(g, 1)
            pool.wait_ge(g, 2)
            nc.gpsimd.tensor_tensor(crs[:], cve[:], chalf[:], ALU.pow).then_inc(crs_ready, 1)

        @block.scalar
        def _(act):
            act.wait_ge(ucs_ready, 1)
            for h in range(2):
                src = ucs[:, h * DH:(h + 1) * DH, :].unsqueeze(3).to_broadcast([3, DH, 2, B])
                last = nc.scalar.copy(u[h][96:99, 0], src)
            last.then_inc(rep_done, 1)

        @block.tensor
        def _(pe):
            pe.wait_ge(pws_ready, 1)
            for c in range(C):
                for k in range(2):
                    nc.tensor.matmul(psw[:, c // 2, (c % 2) * D:(c % 2 + 1) * D], fa[:, k, :], pws[:, k, c, :],
                                     start=(k == 0), stop=(k == 1))
            for c in range(C):
                for k in range(2):
                    last = nc.tensor.matmul(psw[0:NX, 1, D:2 * D], fx[:, k, c, :], pws[:, k, c, :],
                                            start=(c == 0 and k == 0), stop=(c == C - 1 and k == 1))
            last.then_inc(wps_ready, 1)
            pe.wait_ge(powers_ready, 1)
            for G in range(NCG):
                h, n = divmod(G, NCG // 2)
                part = slice(h * NST, (h + 1) * NST)
                for k in range(2):
                    last = nc.tensor.matmul(
                        psk[0:CG * KA, h * 3 + n // 4, (n % 4) * CG * KB:(n % 4 + 1) * CG * KB],
                        zp[part, k, n * CG:(n + 1) * CG].rearrange("n d a -> n (d a)"),
                        zq[part, k, :, n * CG:(n + 1) * CG].rearrange("n b d -> n d b"),
                        start=(k == 0), stop=(k == 1))
            last.then_inc(taps_ready, 1)

        @block.vector
        def _(dve):
            n = [0]

            def step(ins):
                n[0] += 1
                ins.then_inc(d, 1)
                dve.wait_ge(d, n[0])

            def tt(o, a, b, op):
                step(nc.vector.tensor_tensor(o, a, b, op))

            dve.wait_ge(loaded_w, 64)
            tt(fw[:], freq[:, 0], freq[:, 1], ALU.mult)
            nc.vector.tensor_tensor(pws[:], pw[:], fw[:].unsqueeze(2).unsqueeze(3).to_broadcast([FCH, 2, C, D]),
                                    ALU.mult).then_inc(pws_ready, 1)

            dve.wait_ge(loaded_c, 16)
            nc.vector.tensor_tensor(hc[:], cl[:, 0], cl[:, 1], ALU.add).then_inc(hc_ready, 1)
            dve.wait_ge(hc_ready, 1)
            step(nc.vector.bn_stats(cst[:], hc[:]))
            nc.vector.bn_aggr(cmv[:], cst[:]).then_inc(cmv_ready, 1)

            dve.wait_ge(loaded_a, 16)
            are, aim, bm, cm, dl = (ssm[:, i] for i in range(5))
            tt(v[:, 0], are, dl, ALU.mult)
            tt(v[:, 1], aim, dl, ALU.mult)
            step(nc.vector.tensor_scalar(v[:], v[:], 1.0 / 16, None, ALU.mult))

            def cmul(o, a, b):
                nc.vector.tensor_tensor(q[:, 0:2], a[:, 0:1].to_broadcast([128, 2, DH]), b, ALU.mult)
                tt(q[:, 2:4], a[:, 1:2].to_broadcast([128, 2, DH]), b, ALU.mult)
                nc.vector.tensor_tensor(o[:, 0], q[:, 0], q[:, 3], ALU.subtract)
                tt(o[:, 1], q[:, 1], q[:, 2], ALU.add)

            order = 8
            step(nc.vector.tensor_scalar(p[:], v[:], 1.0 / order, None, ALU.mult))
            step(nc.vector.tensor_scalar(p[:, 0], p[:, 0], 1.0, None, ALU.add))
            for k in range(order - 1, 1, -1):
                cmul(p, v, p[:])
                step(nc.vector.tensor_scalar(p[:], p[:], 1.0 / k, None, ALU.mult))
                step(nc.vector.tensor_scalar(p[:, 0], p[:, 0], 1.0, None, ALU.add))
            cmul(e1, v, p[:])
            for _ in range(4):
                nc.vector.tensor_scalar(p[:, 0], e1[:, 0], 2.0, None, ALU.add)
                step(nc.vector.tensor_copy(p[:, 1], e1[:, 1]))
                cmul(e1, e1, p[:])

            nc.vector.tensor_tensor(q[:, 0], are, are, ALU.mult)
            tt(q[:, 1], aim, aim, ALU.mult)
            tt(q[:, 2], q[:, 0], q[:, 1], ALU.add)
            nc.vector.reciprocal(q[:, 3], q[:, 2])
            tt(q[:, 0], bm, cm, ALU.mult)
            step(nc.vector.scalar_tensor_tensor(out=v[:, 0], in0=q[:, 0], scalar=SCALE, in1=q[:, 3],
                                                op0=ALU.mult, op1=ALU.mult))
            nc.vector.tensor_tensor(q[:, 0], e1[:, 0], are, ALU.mult)
            nc.vector.tensor_tensor(q[:, 1], e1[:, 1], aim, ALU.mult)
            nc.vector.tensor_tensor(q[:, 2], e1[:, 1], are, ALU.mult)
            tt(q[:, 3], e1[:, 0], aim, ALU.mult)
            nc.vector.tensor_tensor(q[:, 0], q[:, 0], q[:, 1], ALU.add)
            tt(q[:, 2], q[:, 2], q[:, 3], ALU.subtract)
            nc.vector.tensor_tensor(cf[:, 0], q[:, 0], v[:, 0], ALU.mult)
            tt(cf[:, 1], q[:, 2], v[:, 0], ALU.mult)

            def powers(t, first):
                nc.vector.memset(t[:, :, 0], 0.0)
                step(nc.vector.tensor_copy(t[:, :, 1], first))
                for m, c in ((1, 1), (2, 2), (4, 4), (8, 6)):
                    low, new = t[:, :, 1:1 + c], t[:, :, m + 1:m + 1 + c]
                    shape = [128, 2, c, DH]
                    nc.vector.tensor_tensor(sr[:, :, 0:c], t[:, 0:1, m:m + 1].to_broadcast(shape), low, ALU.mult)
                    nc.vector.tensor_tensor(si[:, :, 0:c], t[:, 1:2, m:m + 1].to_broadcast(shape), low, ALU.mult)
                    tt(new, t[:, :, m:m + 1].to_broadcast(shape), low, ALU.add)
                    tt(new, new, sr[:, :, 0:c], ALU.add)
                    nc.vector.tensor_tensor(new[:, 0], new[:, 0], si[:, 1, 0:c], ALU.subtract)
                    tt(new[:, 1], new[:, 1], si[:, 0, 0:c], ALU.add)

            powers(tq, e1[:])
            powers(tp, tq[:, :, KB])
            nc.vector.tensor_scalar(zq[:, 0], tq[:, 0, KB - 1::-1], 1.0, None, ALU.add)
            nc.vector.tensor_copy(zq[:, 1], tq[:, 1, KB - 1::-1])
            step(nc.vector.tensor_scalar(tp[:, 0], tp[:, 0], 1.0, None, ALU.add))
            shape = [128, 2, KA, DH]
            nc.vector.tensor_tensor(sr[:], cf[:, 0:1].unsqueeze(1).to_broadcast(shape), tp[:], ALU.mult)
            tt(si[:], cf[:, 1:2].unsqueeze(1).to_broadcast(shape), tp[:], ALU.mult)
            nc.vector.tensor_tensor(zp[:, 0].rearrange("p d a -> p a d"), sr[:, 0, ::-1], si[:, 1, ::-1], ALU.subtract)
            nc.vector.scalar_tensor_tensor(out=zp[:, 1].rearrange("p d a -> p a d"), in0=sr[:, 1, ::-1], scalar=-1.0, in1=si[:, 0, ::-1],
                                           op0=ALU.mult, op1=ALU.subtract).then_inc(powers_ready, 1)

            dve.wait_ge(crs_ready, 1)
            step(nc.vector.tensor_scalar(uc[:], hc[:], cmv[:, 0:1], crs[:], ALU.subtract, ALU.mult))
            step(nc.vector.tensor_copy(ucs[:, :, 0], uc[:]))
            nc.vector.tensor_tensor(ucs[:, :, 1], uc[:], ucs[:, :, 0], ALU.subtract).then_inc(ucs_ready, 1)
            dve.wait_ge(wps_ready, 1)
            nc.vector.tensor_scalar(wf[:, 0:2], psw[:, 0, 0:2 * D].rearrange("p (c e) -> p c e", c=2), SCALE, None,
                                    ALU.mult)
            nc.vector.tensor_scalar(wf[:, 2], psw[:, 1, 0:D], SCALE, None, ALU.mult)
            step(nc.vector.tensor_scalar(wxf[:], psw[0:NX, 1, D:2 * D], SCALE, None, ALU.mult))
            nc.vector.tensor_copy(w["hi"][:], wf[:])
            step(nc.vector.tensor_copy(wxh[:], wxf[:]))
            nc.vector.tensor_tensor(w["lo"][:], wf[:], w["hi"][:], ALU.subtract)
            step(nc.vector.scalar_tensor_tensor(out=w["x"][:], in0=wxh[:], scalar=w["signs"][:, 0:1], in1=wxf[:],
                                                op0=ALU.mult, op1=ALU.add))

            dve.wait_ge(taps_ready, 1)
            kfv = kf.rearrange("p g c -> p (g c)").rearrange("p (k c) -> p k c", k=6)
            step(nc.vector.tensor_copy(kfv, psk[0:CG * KA, :, 0:4 * CG * KB]))
            step(nc.vector.tensor_copy(ks[:, :, :, 0], kf))
            nc.vector.tensor_tensor(ks[:, :, :, 1], kf, ks[:, :, :, 0], ALU.subtract).then_inc(split_ready, 1)

            dve.wait_ge(k0_in, 64)
            tt(k0f[:], k0[:, :, 0], k0[:, :, 1], ALU.add)
            nc.vector.scalar_tensor_tensor(out=yc[:], in0=k0f[:], scalar=1.0 / SCALE, in1=uc[0:1, :],
                                           op0=ALU.mult, op1=ALU.mult).then_inc(yc_ready, 1)


def embed(nc, io, u, w, area, resid):
    with ExitStack() as ctx:
        def sb(name, shape, dt=F32):
            return ctx.enter_context(nc.sbuf_tensor(name, shape, dt))

        def sem(name):
            return ctx.enter_context(nc.semaphore(name))

        xa, xb = pixel_tiles(area)
        xe = w["xe"]
        xh = [sb(f"xh{i}", [ROWS, C, GT], F16) for i in range(2)]
        xl = [sb(f"xl{i}", [ROWS, C, GT], F16) for i in range(2)]
        eh = [sb(f"eh{i}", [NX, GT], F16) for i in range(2)]
        es = [sb(f"es{i}", [NX, GT], F16) for i in range(2)]
        add = sb("add", [HALF, 2, D])
        pos = sb("pos", [HALF, 2, D])
        h = [sb(f"h{i}", [HALF, GI, 2, D]) for i in range(2)]
        un = sb("un", [HALF, GI, 2, D])
        uh = sb("uh", [HALF, GI, 2, D], F16)
        st = sb("st", [HALF, GI * 2, 6])
        mv = sb("mv", [HALF, GI * 2, 2])
        ve = sb("ve", [HALF, GI * 2, 1])
        rs = sb("rs", [HALF, GI * 2, 1])
        mhalf = sb("mhalf", [HALF, GI * 2, 1])
        eps = sb("eps", [HALF, GI * 2, 1])
        minus = sb("minus", [HALF, GI * 2, 1])
        neg = sb("neg", [HALF, GI * 2, 1])
        nb = sb("nb", [HALF, GI * 2, 1])
        ps = ctx.enter_context(nc.psum_tensor("ps", [HALF, 2 * GI, 512], F32))

        names = ("pos_in", "folded", "xh_ready", "xl_ready", "eh_ready", "es_ready", "tokens_ready",
                 "h_ready", "stats_ready", "mv_ready", "ve_ready", "rs_ready", "const_ready", "un_ready",
                 "uh_ready", "ul_d", "ul_p", "u_copied", "h_out0", "h_out1", "add_ready")
        s = {name: sem(name) for name in names}
        s.update({f"x_in{i}": w["x_in"][i] for i in range(2)})
        block = ctx.enter_context(nc.Block())
        PAIRS = NG // 2

        def low_u(engine, queue, done, n, g):
            queue.wait_ge(s["uh_ready"], g + 1)
            for k in range(2):
                last = engine.tensor_tensor(u[n][0:HALF, k, :, 1, bass.ds(GI * g, GI)],
                                            un[:, :, k, n * DH:(n + 1) * DH].rearrange("p b d -> p d b"),
                                            uh[:, :, k, n * DH:(n + 1) * DH].rearrange("p b d -> p d b"),
                                            ALU.subtract)
            last.then_inc(s[done], 1)

        @block.sync
        def _(sp):
            sp.dma_start(add[:], io["pos"][0]).then_inc(s["pos_in"], 16)
            sp.dma_start(pos[:], io["pos"][1]).then_inc(s["pos_in"], 16)

            with sp.Fori(1, PAIRS) as j:
                for i in range(2):
                    g = 2 * j + i
                    sp.wait_ge(s["xl_ready"], g - 1)
                    sp.wait_ge(s["es_ready"], g - 1)
                    load_pixels(sp, io, w, area, g, i)

        @block.scalar
        def _(act):
            def split(g, i):
                act.wait_ge(s[f"x_in{i}"], 24 * (g - i) + 48)
                nc.scalar.copy(eh[i][:], xe[i][:]).then_inc(s["eh_ready"], 1)
                for c in range(C):
                    act.wait_ge(s["folded"], C * g + c + 1)
                    nc.scalar.copy(xh[i][:, c], xa[i][:, c]).then_inc(s["xh_ready"], 1)

            def store(g, i):
                act.wait_ge(s["h_ready"], GI * (g + 1))
                rows = resid.rearrange("(b l) d -> b l d", l=SEQ)[bass.ds(GI * g, GI), 1:SEQ]
                for k in range(2):
                    act.dma_start(rows[:, k * HALF:(k + 1) * HALF].rearrange("b l d -> l b d"),
                                  h[i][:, :, k]).then_inc(s[f"h_out{i}"], 16)

            def normal(g, i):
                act.wait_ge(s["rs_ready"], g + 1)
                act.wait_ge(s["ul_d"], g + 1)
                act.wait_ge(s["ul_p"], g + 1)
                act.wait_ge(s["u_copied"], 4 * g + 4)
                for n in range(2 * GI):
                    last = nc.scalar.activation(un[:, n // 2, n % 2], h[i][:, n // 2, n % 2], ACT.Identity,
                                                bias=nb[:, n], scale=rs[:, n])
                last.then_inc(s["un_ready"], 1)
                act.wait_ge(s["un_ready"], g + 2)
                nc.scalar.copy(uh[:], un[:]).then_inc(s["uh_ready"], 1)
                act.wait_ge(s["uh_ready"], g + 1)
                for n in range(2):
                    for k in range(2):
                        nc.scalar.copy(u[n][0:HALF, k, :, 0, bass.ds(GI * g, GI)],
                                       uh[:, :, k, n * DH:(n + 1) * DH].rearrange("p b d -> p d b")
                                       ).then_inc(s["u_copied"], 1)

            split(0, 0)
            split(1, 1)
            store(0, 0)
            with act.Fori(1, PAIRS) as j:
                for i in range(2):
                    g = 2 * j + i
                    act.wait_ge(s["tokens_ready"], GI * (g - 1))
                    split(g, i)
                    normal(g - 2, i)
                    store(g - 1, 1 - i)
            normal(NG - 2, 0)
            store(NG - 1, 1)
            normal(NG - 1, 1)
            for i in range(2):
                act.wait_ge(s[f"h_out{i}"], 16 * NG + 16)

        @block.gpsimd
        def _(pool):
            nc.gpsimd.memset(mhalf[:], -0.5).then_inc(s["const_ready"], 1)
            nc.gpsimd.memset(eps[:], EPS).then_inc(s["const_ready"], 1)
            nc.gpsimd.memset(minus[:], -1.0).then_inc(s["const_ready"], 1)
            pool.wait_ge(s["const_ready"], 3)

            def low(g, i):
                for c in range(C):
                    pool.wait_ge(s["xh_ready"], C * g + c + 1)
                    last = nc.gpsimd.tensor_tensor(xl[i][:, c], xa[i][:, c], xh[i][:, c], ALU.subtract)
                last.then_inc(s["xl_ready"], 1)

            def rstd(g):
                pool.wait_ge(s["mv_ready"], g + 1)
                nc.gpsimd.tensor_tensor(ve[:], mv[:, :, 1:2], eps[:], ALU.add).then_inc(s["ve_ready"], 1)
                pool.wait_ge(s["ve_ready"], 3 * g + 1)
                nc.gpsimd.tensor_tensor(rs[:], ve[:], mhalf[:], ALU.pow).then_inc(s["ve_ready"], 1)
                nc.gpsimd.tensor_tensor(neg[:], mv[:, :, 0:1], minus[:], ALU.mult).then_inc(s["ve_ready"], 1)
                pool.wait_ge(s["ve_ready"], 3 * g + 3)
                nc.gpsimd.tensor_tensor(nb[:], neg[:], rs[:], ALU.mult).then_inc(s["rs_ready"], 1)

            low(0, 0)
            low(1, 1)
            rstd(0)
            with pool.Fori(1, PAIRS) as j:
                for i in range(2):
                    low(2 * j + i, i)
                    low_u(nc.gpsimd, pool, "ul_p", 1, 2 * j + i - 2)
                    rstd(2 * j + i - 1)
            low_u(nc.gpsimd, pool, "ul_p", 1, NG - 2)
            rstd(NG - 1)
            low_u(nc.gpsimd, pool, "ul_p", 1, NG - 1)

        @block.tensor
        def _(pe):
            def tokens(g, i, guarded):
                pe.wait_ge(s["xl_ready"], g + 1)
                pe.wait_ge(s["es_ready"], g + 1)
                for m in range(GI):
                    bank = GI * i + m
                    if guarded:
                        pe.wait_ge(s["h_ready"], GI * (g - 2) + m + 1)
                    for k in range(2):
                        out = ps[:, bank, k * D:(k + 1) * D]
                        t = slice((2 * m + k) * HALF, (2 * m + k + 1) * HALF)
                        nc.tensor.matmul(out, es[i][:, t], w["x"][:], start=True, stop=False)
                        for c in range(C):
                            nc.tensor.matmul(out, xh[i][:, c, t], w["hi"][:, c], start=False, stop=False)
                            nc.tensor.matmul(out, xh[i][:, c, t], w["lo"][:, c], start=False, stop=False)
                            last = nc.tensor.matmul(out, xl[i][:, c, t], w["hi"][:, c], start=False, stop=(c == C - 1))
                    last.then_inc(s["tokens_ready"], 1)

            for i in range(2):
                tokens(i, i, False)
            with pe.Fori(1, PAIRS) as j:
                for i in range(2):
                    tokens(2 * j + i, i, True)

        @block.vector
        def _(dve):
            dve.wait_ge(s["pos_in"], 32)
            nc.vector.tensor_tensor(add[:], add[:], pos[:], ALU.add).then_inc(s["add_ready"], 1)
            dve.wait_ge(s["add_ready"], 1)

            def fold(g, i):
                dve.wait_ge(s[f"x_in{i}"], 24 * (g - i) + 48)
                for c in range(C):
                    nc.vector.tensor_tensor(xa[i][:, c], xa[i][:, c], xb[i][:, c], ALU.add).then_inc(s["folded"], 1)

            def low_rows(g, i):
                dve.wait_ge(s["eh_ready"], g + 1)
                nc.vector.scalar_tensor_tensor(out=es[i][:], in0=eh[i][:], scalar=w["signs"][:, 1:2], in1=xe[i][:],
                                               op0=ALU.mult, op1=ALU.add).then_inc(s["es_ready"], 1)

            def finish(g, i, guarded):
                if guarded:
                    dve.wait_ge(s[f"h_out{i}"], 16 * (g - i) + 16)
                    dve.wait_ge(s["un_ready"], g)
                    dve.wait_ge(s["rs_ready"], g)
                for m in range(GI):
                    dve.wait_ge(s["tokens_ready"], GI * g + m + 1)
                    nc.vector.scalar_tensor_tensor(
                        out=h[i][:, m].rearrange("p k d -> p (k d)"), in0=ps[:, GI * i + m, 0:2 * D],
                        scalar=1.0 / SCALE, in1=add[:].rearrange("p k d -> p (k d)"),
                        op0=ALU.mult, op1=ALU.add).then_inc(s["h_ready"], 1)
                dve.wait_ge(s["h_ready"], GI * (g + 1))
                for n in range(2 * GI):
                    last = nc.vector.bn_stats(st[:, n], h[i][:, n // 2, n % 2])
                last.then_inc(s["stats_ready"], 1)
                dve.wait_ge(s["pos_in"], 32)
                dve.wait_ge(s["stats_ready"], g + 1)
                for n in range(2 * GI):
                    last = nc.vector.bn_aggr(mv[:, n], st[:, n])
                last.then_inc(s["mv_ready"], 1)

            for i in range(2):
                dve.sem_inc(s[f"h_out{i}"], 16)
            for name, value in (("un_ready", 1), ("ul_d", 1), ("ul_p", 1), ("u_copied", 4)):
                dve.sem_inc(s[name], value)
            fold(0, 0)
            low_rows(0, 0)
            fold(1, 1)
            low_rows(1, 1)
            finish(0, 0, False)
            with dve.Fori(1, PAIRS) as j:
                for i in range(2):
                    g = 2 * j + i
                    fold(g, i)
                    low_rows(g, i)
                    finish(g - 1, 1 - i, True)
                    low_u(nc.vector, dve, "ul_d", 0, g - 2)
            low_u(nc.vector, dve, "ul_d", 0, NG - 2)
            finish(NG - 1, 1, True)
            low_u(nc.vector, dve, "ul_d", 0, NG - 1)


def store_mixed(queue, y, mixed, n, done, first, last):
    for q in range(2):
        rows = mixed[2 * n + q].rearrange("(b l) d -> b (l d)", l=SEQ)[first:last, DQ:SEQ * DQ]
        queue.dma_start(rows, y[q * B + first:q * B + last].rearrange("p l d -> p (l d)")).then_inc(done, 16)


def mix(nc, u, area, y_stored, taps, mixed):
    with ExitStack() as ctx:
        def sb(name, shape, dt=F32):
            return ctx.enter_context(nc.sbuf_tensor(name, shape, dt))

        def sem(name):
            return ctx.enter_context(nc.semaphore(name))

        CQ = CG // 2
        t = [sb(f"toeplitz{i}", [HALF + 1, 2, CQ, TC, 2], F16) for i in range(2)]
        ug = [sb(f"ug{i}", [HALF + 1, 2, 2, CQ, 2, B], F16) for i in range(2)]
        y = [sb("y", [128, NPATCH, DQ]), area[:, 0:NPATCH * DQ].rearrange("p (l d) -> p l d", l=NPATCH)]
        ps = ctx.enter_context(nc.psum_tensor("conv", [128, 4, 512], F32))
        names = ("t_in0", "t_in1", "u_ready", "u2_ready", "conv0", "conv1", "y0", "y1", "y_out")
        t_in0, t_in1, u_ready, u2_ready, conv0, conv1, y0, y1, y_out = (sem(n) for n in names)
        block = ctx.enter_context(nc.Block())
        HG = NCG // 2
        t_in = (t_in0, t_in1)

        @block.sync
        def _(sp):
            def load(n, i, guarded):
                if guarded:
                    sp.wait_ge(conv1, n - 1)
                sp.dma_start(t[i][0:HALF].rearrange("p q c t k -> p (q c) (t k)"),
                             bass.AP(taps.tensor, n * (CG * RW * 2) + 2 * (SKIP + 1),
                                     [(2, HALF), (RW * 2, CG), (1, TC * 2)])).then_inc(t_in[i], 16)
                sp.dma_start(t[i][HALF:HALF + 1].rearrange("p q c t k -> p (q c) (t k)"),
                             bass.AP(taps.tensor, n * (CG * RW * 2) + 2 * SKIP,
                                     [(RW * 2 * D, 1), (RW * 2, CG), (1, TC * 2)])).then_inc(t_in[i], 16)

            load(0, 0, False)
            load(1, 1, False)
            with sp.Fori(1, NCG // 2) as j:
                for i in range(2):
                    load(2 * j + i, i, True)

        def gather(eng, copy, half, ready):
            def group(n, i, un):
                if not (isinstance(n, int) and n < 2):
                    eng.wait_ge(conv1, n - 1)
                rows = HALF + 1 - half
                for q in range(2):
                    at = (n - un * HG) * CQ + q * DQ
                    last = copy(ug[i][0:rows, half, q], u[un][0:rows, half, bass.ds(at, CQ)])
                last.then_inc(ready, 1)
            return group

        @block.gpsimd
        def _(pool):
            group = gather(pool, nc.gpsimd.tensor_copy, 1, u2_ready)
            group(0, 0, 0)
            group(1, 1, 0)
            with pool.Fori(1, HG // 2) as j:
                for i in range(2):
                    group(2 * j + i, i, 0)
            with pool.Fori(HG // 2, NCG // 2) as j:
                for i in range(2):
                    group(2 * j + i, i, 1)

        @block.tensor
        def _(pe):
            def group(n, i, guarded):
                pe.wait_ge(t_in[i], 16 * (n - i) + 32)
                pe.wait_ge(u_ready, n + 1)
                pe.wait_ge(u2_ready, n + 1)
                parts = ((0, 0), (1, 0), (0, 1))
                for bank, (done, used) in enumerate(((conv0, y0), (conv1, y1))):
                    if guarded:
                        pe.wait_ge(used, n - 1)
                    for c in range(2 * bank, 2 * bank + 2):
                        for a, (kk, uu) in enumerate(parts):
                            for q in range(2):
                                col = (c % 2) * TC
                                o = ps[q * B:(q + 1) * B, 2 * i + bank, col:col + TC]
                                nc.tensor.matmul(o, ug[i][:, 0, q, c, uu], t[i][:, q, c, ::-1, kk],
                                                 start=(a == 0), stop=False)
                        for a, (kk, uu) in enumerate(parts):
                            for q in range(2):
                                o = ps[q * B:(q + 1) * B, 2 * i + bank, col + HALF:col + TC]
                                last = nc.tensor.matmul(o, ug[i][0:HALF, 1, q, c, uu],
                                                        t[i][0:HALF, q, c, ::-1, kk][:, 0:HALF],
                                                        start=False, stop=(a == 2))
                    last.then_inc(done, 1)

            group(0, 0, False)
            group(1, 1, False)
            with pe.Fori(1, NCG // 2) as j:
                for i in range(2):
                    group(2 * j + i, i, True)

        def copy_out(eng, do, bank, done, ready, n, i, un):
            eng.wait_ge(ready, n + 1)
            at = (n - un * HG) * CQ + 2 * bank
            do(y[un][:, :, bass.ds(at, 2)].rearrange("p l c -> p c l"),
               ps[:, 2 * i + bank, 0:2 * TC].rearrange("p (c l) -> p c l", c=2)).then_inc(done, 1)

        @block.scalar
        def _(act):
            def scaled(o, a):
                return nc.scalar.mul(o, a, 1.0 / SCALE)

            def store(n, done, first, last):
                store_mixed(act, y[n], mixed, n, done, first, last)

            with act.Fori(0, HG // 2) as j:
                for i in range(2):
                    copy_out(act, scaled, 0, y0, conv0, 2 * j + i, i, 0)
            act.wait_ge(y0, HG)
            act.wait_ge(y1, HG)
            store(0, y_out, 0, B)
            with act.Fori(HG // 2, NCG // 2) as j:
                for i in range(2):
                    copy_out(act, scaled, 0, y0, conv0, 2 * j + i, i, 1)
            act.wait_ge(y_out, 32)
            act.wait_ge(y0, NCG)
            act.wait_ge(y1, NCG)
            store(1, y_stored, 0, FIRST_IMAGES)

        @block.vector
        def _(dve):
            def scaled(o, a):
                return nc.vector.tensor_scalar(o, a, 1.0 / SCALE, None, ALU.mult)

            group = gather(dve, nc.vector.tensor_copy, 0, u_ready)
            group(0, 0, 0)
            group(1, 1, 0)
            with dve.Fori(1, HG // 2) as j:
                for i in range(2):
                    copy_out(dve, scaled, 1, y1, conv1, 2 * j + i - 2, i, 0)
                    group(2 * j + i, i, 0)
            for i in range(2):
                copy_out(dve, scaled, 1, y1, conv1, HG - 2 + i, i, 0)
                group(HG + i, i, 1)
            with dve.Fori(HG // 2 + 1, NCG // 2) as j:
                for i in range(2):
                    copy_out(dve, scaled, 1, y1, conv1, 2 * j + i - 2, i, 1)
                    group(2 * j + i, i, 1)
            for i in range(2):
                copy_out(dve, scaled, 1, y1, conv1, NCG - 2 + i, i, 1)


def feed_forward(nc, io, area, y_stored, resid, mixed, routed, out):
    with ExitStack() as ctx:
        t = {"w": [ctx.enter_context(nc.sbuf_tensor(f"ffn_w_{n}", [128, W_COLS], F16)) for n in ("hi", "lo")],
             "ident": ctx.enter_context(nc.sbuf_tensor("ident", [128, 128], F16)),
             "units": ctx.enter_context(nc.sbuf_tensor("units", [128, 2, NU], U32)),
             "expert": ctx.enter_context(nc.sbuf_tensor("expert", [128, NU], F32)),
             "pairs": ctx.enter_context(nc.sbuf_tensor("pairs", [128, 1], U32))}
        shared_expert(nc, io, t, area, y_stored, resid, mixed, routed, out)
        routed_experts(nc, t, routed, out)


def shared_expert(nc, io, t, area, y_stored, resid, mixed, routed, out):
    with ExitStack() as ctx:
        def sb(name, shape, dt=F32):
            return ctx.enter_context(nc.sbuf_tensor(name, shape, dt))

        def sem(name):
            return ctx.enter_context(nc.semaphore(name))

        w, ident = t["w"], t["ident"]
        wa = [x[:, 0:2 * HS].rearrange("p (k h) -> p k h", k=2) for x in w]
        wb = [x[:, 2 * HS:4 * HS].rearrange("p (k h) -> p k h", k=2) for x in w]
        wd = [x[:, 4 * HS:W_SHARED].rearrange("p (m d) -> p m d", m=NSH) for x in w]
        wr = [sb(f"wr_{n}", [128, 2, E + 1], F16) for n in ("hi", "lo")]
        wrf = sb("wrf", [128, 2, E + 1])
        tri = sb("tri", [128, 128], F16)
        ones = sb("ones", [128, 128], F16)
        ids = sb("ids", [128, (NBLK + 1) * NT], U32)
        fields, width = table_fields()
        ctab = sb("ctab", [128, width])

        def const(name, shape="p n -> p n", **kw):
            at, n = fields[name]
            return ctab[:, at:at + n].rearrange(shape, **kw)

        valid, far = (const(n, "p (k t) -> p k t", k=2) for n in ("valid", "far"))
        iota = sb("iota", [128, NT, E])
        sgb = sb("sgb", [128, NT, E + 1])
        mhalf = sb("mhalf2", [128, NT, 1])
        eps = sb("eps2", [128, NT, 1])
        cuts = [n * W_SHARED // 4 for n in range(4)] + [W_SHARED + e * W_EXPERT for e in range(E + 1)]
        pieces = [(lo, hi - lo) for lo, hi in zip(cuts, cuts[1:])]
        stage = [sb(f"stage{i}", [128, W_EXPERT]) for i in range(2)]
        LATER = {0: (4, 5, 6), NBLK - 2: (7, 8, 9), NBLK - 1: (10, 11)}

        def staged_at(b, m):
            late = LATER.get(b, ()) if isinstance(b, int) else ()
            return late[m // 2:m // 2 + 1] if m % 2 else ()

        hin = [sb(f"hin{i}", [128, NT, D]) for i in range(2)]
        yin = [sb(f"yin{i}", [128, NT, D]) for i in range(2)]
        h2 = [sb(f"h2_{i}", [128, NT, D]) for i in range(2)]
        ot = [sb(f"ot{i}", [128, NT, D]) for i in range(2)]
        st = sb("st2", [128, NT, 6])
        mv = sb("mv2", [128, NT, 2])
        ve = sb("ve2", [128, NT, 1])
        rs = sb("rs2", [128, NT, 1])
        xn = sb("xn", [128, NT, D])
        rows_w = [sb(f"rows_w{i}", [128, NT, RX // 2], U32) for i in range(2)]
        xs = [x[:].bitcast(F16)[:, :, 0:XW] for x in rows_w]
        words = [x[:, :, XW // 2:RX // 2] for x in rows_w]
        fill = sb("fill", [128, NT, RX // 2], U32)
        xt = [sb(f"xt{i}", [128, 3, BT], F16) for i in range(2)]
        lg = sb("lg", [128, NT, E + 1])
        m8 = sb("m8", [128, NT, 8])
        ix = sb("ix", [128, NT, 8], U32)
        ixf = sb("ixf", [128, NT, 2])
        z = sb("z", [128, NT, 2])
        th = sb("th", [128, NT, 2])
        ga = sb("ga", [128, NT, 2])
        gb = sb("gb", [128, NT, 2])
        alpha = [sb(f"alpha{i}", [128, NT]) for i in range(2)]
        hot = sb("hot", [128, 2, NT, E])
        both = sb("both", [128, NT, E])
        oh = sb("oh", [128, NT + 1, E], F16)
        gd = sb("gd", [128, NT, 2])
        carry = sb("carry", [128, 1])
        base = sb("base", [128, E])
        rank = sb("rank", [128, NT, E])
        pick = sb("pick", [128, 2, NT, E])
        slotf = sb("slotf", [128, 2, NT])
        slot = [sb(f"slot{i}", [128, 2, NT], U32) for i in range(2)]
        base_u = sb("base_u", [128, E], U32)
        count = sb("count", [128, E])
        over = sb("over", [128, E, NBLK])
        units = sb("units_of", [128, E])
        starts = sb("starts", [128, E + 1, E])
        start = sb("start", [128, E + 1])
        jump = sb("jump", [128, E + 1])
        ge = sb("ge", [128, NU, E + 1])
        gj = sb("gj", [128, NU, E + 1])
        rowf = sb("rowf", [128, NU])
        colf = sb("colf", [128, NU])
        pairs2 = sb("pairs2", [128, NU // 2])
        pairf = sb("pairf", [128, 1])
        sg = [sb(f"sg{i}", [128, BT]) for i in range(2)]
        hf = [sb(f"hf{i}", [128, BT]) for i in range(2)]
        hh = [sb(f"hh{i}", [128, BT], F16) for i in range(2)]
        hl = [sb(f"hl{i}", [128, BT], F16) for i in range(2)]

        psg = ctx.enter_context(nc.psum_tensor("psg", [128, 2, 512], F32))
        psu = ctx.enter_context(nc.psum_tensor("psu", [128, 2, 512], F32))
        psx = ctx.enter_context(nc.psum_tensor("psx", [128, 2, 512], F32))
        pso = ctx.enter_context(nc.psum_tensor("pso", [128, 2, 512], F32))
        px16 = [psx[:, i].bitcast(F16) for i in range(2)]

        names = ("const_in", "mixed_out", "stage_in0", "stage_in1", "oh_ready", "rank_ps", "slots_ready",
                 "sent0", "sent1", "base_set", "table", "fill_ready", "base_ready", "fillers", "stage_hi", "stage_lo", "wrf_hi", "wr_ready", "memsets",
                 "rows_in0", "rows_in1", "h2_ready", "stats_ready", "mv_ready", "ve_ready", "rs_ready", "xn_ready",
                 "xhi_ready", "xlo_ready", "xt_ps", "xt_0", "xt_a", "lg_ps", "lg_ready", "route", "th_ready",
                 "g_ps", "u_ps", "sg_ready", "hf_ready",
                 "hh_ready", "hl_ready", "down", "kept", "out_ready", "stored0", "stored1")
        s = {name: sem("b_" + name) for name in names}
        block = ctx.enter_context(nc.Block())
        LOOPS = (NBLK - 3) // 2
        ROUTE = 14
        SENT = 32 * NT
        SHIFT = LAST_START

        def schedule(eng, body):
            body(0, 0, NT, NT)
            with eng.Fori(0, LOOPS) as j:
                for i in range(2):
                    body(2 * j + 1 + i, 1 - i, NT, NT)
            body(NBLK - 2, (NBLK - 2) % 2, NT, LAST_NT)
            body(NBLK - 1, (NBLK - 1) % 2, LAST_NT, 0)

        def rows(dram, b, nt):
            at = b * BT if nt == NT else SHIFT
            return dram[bass.ds(at, nt * 128)].rearrange("(t p) d -> p t d", p=128)

        def is_first(b):
            return isinstance(b, int) and b == 0

        @block.sync
        def _(sp):
            consts = ((wrf, "w_r"), (ident, "ident"), (tri, "tri"), (iota, "iota"), (sgb, "sgb"), (ids, "ids"),
                      (ctab, "ctab"))
            for dst, src in consts:
                sp.dma_start(dst[:], io[src][:]).then_inc(s["const_in"], 16)

            def load(b, q, nt):
                sp.dma_start(hin[q][:, 0:nt], rows(resid, b, nt)).then_inc(s[f"rows_in{q}"], 16)
                for c in range(4):
                    sp.dma_start(yin[q][:, 0:nt, c * DQ:(c + 1) * DQ],
                                 rows(mixed[c], b, nt)).then_inc(s[f"rows_in{q}"], 16)

            def stage_in(n):
                if n >= 2:
                    sp.wait_ge(s["stage_lo"], n - 1)
                at, width = pieces[n]
                sp.dma_start(stage[n % 2][:, 0:width], io["w_all"][:, at:at + width]).then_inc(s[f"stage_in{n % 2}"], 16)

            stage_in(0)
            stage_in(1)
            sp.wait_ge(y_stored, 32)
            load(0, 0, NT)
            load(1, 1, NT)
            stage_in(2)
            stage_in(3)
            y = area[:, 0:NPATCH * DQ].rearrange("p (l d) -> p l d", l=NPATCH)
            store_mixed(sp, y, mixed, 1, s["mixed_out"], FIRST_IMAGES, B)
            stage_in(4)
            stage_in(5)

            def body(b, q, nt, nn):
                if not (isinstance(b, int) and b >= NBLK - 3) :
                    sp.wait_ge(s["h2_ready"], b + 1)
                    load(b + 2, q, NT)

            sp.wait_ge(s["mixed_out"], 32)
            body(0, 0, NT, NT)
            for n in (6, 7, 8):
                stage_in(n)
            with sp.Fori(0, LOOPS - 1) as j:
                for i in range(2):
                    body(2 * j + 1 + i, 1 - i, NT, NT)
            body_last = ((NBLK - 4, NT), (NBLK - 3, LAST_NT))
            for b, nt in body_last:
                sp.wait_ge(s["h2_ready"], b + 1)
                load(b + 2, b % 2, nt)

            for n in (9, 10, 11):
                stage_in(n)

            sp.wait_ge(s["fill_ready"], 1)
            for n in range(NFILL):
                sp.dma_start(routed[FILL + n * UNIT:FILL + (n + 1) * UNIT].rearrange("(t p) d -> p t d", p=128),
                             fill[:]).then_inc(s["fillers"], 16)
            sp.dma_start(out[NTOK:OUT_ROWS].rearrange("(t p) d -> p t d", p=128),
                         fill[:, :, 0:XW // 2].bitcast(F32)).then_inc(s["fillers"], 16)
            sp.wait_ge(s["base_ready"], 1)
            for e in range(E):
                at = nc.sync.value_load(base_u[0:1, e:e + 1], min_val=e * CAP, max_val=e * CAP + NTOK)
                sp.dma_start(routed[bass.ds(at, UNIT)].rearrange("(t p) d -> p t d", p=128),
                             fill[:]).then_inc(s["fillers"], 16)
            sp.wait_ge(s["fillers"], 16 * (NFILL + 1 + E))

        def chunk_sem(b, m):
            return NSH * b + m

        @block.tensor
        def _(pe):
            def transposes(b, q, nt):
                pe.wait_ge(s["xlo_ready"], b + 1)
                if not is_first(b):
                    pe.wait_ge(s["slots_ready"], b)
                for c in range(3):
                    for t in range(nt):
                        o = px16[c // 2][:, (c % 2) * BT + t * 128:(c % 2) * BT + (t + 1) * 128]
                        last = nc.tensor.transpose(o, xs[q][:, t, c * 128:(c + 1) * 128], ident[:])
                    if c:
                        last.then_inc(s["xt_ps"], 1)

            def router(b, q, nt):
                pe.wait_ge(s["xt_0"], b + 1)
                pe.wait_ge(s["xt_a"], b + 1)
                for t in range(nt):
                    o = psx[:, 1, 256 + 16 * t:256 + 16 * t + E + 1]
                    ts = slice(t * 128, (t + 1) * 128)
                    prods = ((0, wr[0][:, 0]), (0, wr[1][:, 0]), (2, wr[0][:, 0]), (1, wr[0][:, 1]), (1, wr[1][:, 1]))
                    for a, (c, r) in enumerate(prods):
                        last = nc.tensor.matmul(o, xt[q][:, c, ts], r, start=(a == 0), stop=(a == 4))
                last.then_inc(s["lg_ps"], 1)

            def ranks(b, q, nt):
                pe.wait_ge(s["oh_ready"], b + 1)
                o = psx[:, 1, 384:384 + (NT + 1) * E]
                flat = oh[:].rearrange("p t e -> p (t e)")
                for k in range(NT, 0, -1):
                    nc.tensor.matmul(o[:, k * E:(NT + 1) * E], ones[:], flat[:, 0:(NT + 1 - k) * E],
                                     start=(k == NT), stop=False, skip_group_check=True)
                last = nc.tensor.matmul(o, tri[:], flat, start=False, stop=True, skip_group_check=True)
                last.then_inc(s["rank_ps"], 1)

            def up(b, q, nt, nn, m):
                n = nt * 128
                if m >= 2 or not is_first(b):
                    pe.wait_ge(s["hf_ready"], chunk_sem(b, m) - 1)
                for k, (ps, done) in enumerate(((psg, "g_ps"), (psu, "u_ps"))):
                    cols = slice(m * 128, (m + 1) * 128)
                    prods = ((wa[0], 0), (wa[1], 0), (wa[0], 2), (wb[0], 1), (wb[1], 1))
                    for a, (wt, c) in enumerate(prods):
                        last = nc.tensor.matmul(ps[:, m % 2, 0:n], wt[:, k, cols], xt[q][:, c, 0:n],
                                                start=(a == 0), stop=(a == 4))
                    last.then_inc(s[done], 1)

            def down(b, nt, m):
                pe.wait_ge(s["hl_ready"], chunk_sem(b, m) + 1)
                if m == 0 and not is_first(b):
                    pe.wait_ge(s["out_ready"], b)
                for t in range(nt):
                    o = pso[:, t // 2, (t % 2) * D:(t % 2 + 1) * D]
                    ts = slice(t * 128, (t + 1) * 128)
                    prods = ((hh, 0), (hh, 1), (hl, 0))
                    for a, (hx, k) in enumerate(prods):
                        last = nc.tensor.matmul(o, hx[m % 2][:, ts], wd[k][:, m],
                                                start=(a == 0 and m == 0 and t % 2 == 0),
                                                stop=(a == 2 and m == NSH - 1), skip_group_check=True)
                last.then_inc(s["down"], 1)

            pe.wait_ge(s["const_in"], 112)
            pe.wait_ge(s["wr_ready"], 1)
            pe.wait_ge(s["memsets"], 5)
            transposes(0, 0, NT)
            router(0, 0, NT)
            ranks(0, 0, NT)
            pe.wait_ge(s["stage_lo"], 4)

            def body(b, q, nt, nn):
                for m in range(NSH):
                    up(b, q, nt, nn, m)
                    if m >= 2:
                        down(b, nt, m - 2)
                    elif not is_first(b):
                        down(b - 1, NT, NSH - 2 + m)
                    if nn and m == 3:
                        transposes(b + 1, 1 - q, nn)
                    if nn and m == 4:
                        router(b + 1, 1 - q, nn)
                    if nn and m == 5:
                        ranks(b + 1, 1 - q, nn)

            schedule(pe, body)
            for m in (NSH - 2, NSH - 1):
                down(NBLK - 1, LAST_NT, m)

        @block.scalar
        def _(act):
            act.wait_ge(s["const_in"], 112)
            nc.scalar.mul(wrf[:], wrf[:], SCALE).then_inc(s["wrf_hi"], 1)
            act.wait_ge(s["wrf_hi"], 1)
            nc.scalar.copy(wr[0][:], wrf[:]).then_inc(s["wrf_hi"], 1)

            def x_high(b, q, nt):
                act.wait_ge(s["xn_ready"], b + 1)
                if not is_first(b):
                    act.wait_ge(s["xt_ps"], 2 * b)
                    if not isinstance(b, int) or b >= 2:
                        act.wait_ge(s[f"sent{q}"], SENT // 2 * (b - q))
                nc.scalar.copy(xs[q][:, 0:nt, 0:D], xn[:, 0:nt]).then_inc(s["xhi_ready"], 1)

            def x_out(b, q, nt):
                n = nt * 128
                act.wait_ge(s["xt_ps"], 2 * b + 1)
                nc.scalar.copy(xt[q][:, 0:2, 0:n],
                               px16[0][:, 0:2 * BT].rearrange("p (c n) -> p c n", c=2)[:, :, 0:n]
                               ).then_inc(s["xt_0"], 1)
                act.wait_ge(s["xt_ps"], 2 * b + 2)
                nc.scalar.copy(xt[q][:, 2, 0:nt * 128], px16[1][:, 0:nt * 128]).then_inc(s["xt_a"], 1)

            def tanh(b, nt):
                act.wait_ge(s["route"], ROUTE * b + 3)
                nc.scalar.activation(th[:, 0:nt], z[:, 0:nt], ACT.Tanh, scale=0.5).then_inc(s["th_ready"], 1)

            def silu(b, nt, m):
                n = nt * 128
                act.wait_ge(s["g_ps"], chunk_sem(b, m) + 1)
                if m >= 2 or not is_first(b):
                    act.wait_ge(s["hf_ready"], chunk_sem(b, m) - 1)
                nc.scalar.activation(sg[m % 2][:, 0:n], psg[:, m % 2, 0:n], ACT.Silu,
                                     scale=1.0 / SCALE).then_inc(s["sg_ready"], 1)

            def high(b, nt, m, first=False):
                n = nt * 128
                act.wait_ge(s["hf_ready"], chunk_sem(b, m) + 1)
                if not first:
                    act.wait_ge(s["down"], chunk_sem(b, m) - 1)
                nc.scalar.copy(hh[m % 2][:, 0:n], hf[m % 2][:, 0:n]).then_inc(s["hh_ready"], 1)

            def keep(b, q, nt):
                act.wait_ge(s["h2_ready"], b + 1)
                act.wait_ge(s[f"stored{q}"], 8 * (b - q) + 16)
                nc.scalar.copy(ot[q][:, 0:nt], h2[q][:, 0:nt]).then_inc(s["kept"], 1)

            def store(b, q, nt):
                act.wait_ge(s["out_ready"], b + 1)
                if nt == LAST_NT:
                    for i in range(2):
                        act.wait_ge(s[f"stored{i}"], 8 * b + 16)
                act.dma_start(rows(out, b, nt), ot[q][:, 0:nt]).then_inc(s[f"stored{q}"], 16)

            def stage_high(n):
                at, width = pieces[n]
                act.wait_ge(s[f"stage_in{n % 2}"], 16 * (n // 2 + 1))
                nc.scalar.mul(w[0][:, at:at + width], stage[n % 2][:, 0:width], SCALE).then_inc(s["stage_hi"], 1)

            for n in range(4):
                stage_high(n)
            x_high(0, 0, NT)
            x_out(0, 0, NT)
            tanh(0, NT)

            def body(b, q, nt, nn):
                for m in range(NSH):
                    silu(b, nt, m)
                    if m >= 1:
                        high(b, nt, m - 1, first=is_first(b) and m - 1 < 2)
                    elif not is_first(b):
                        high(b - 1, NT, NSH - 1)
                    if m == 2 and not is_first(b):
                        store(b - 1, 1 - q, NT)
                    if m == 4:
                        keep(b, q, nt)
                    if nn and m == 2:
                        x_high(b + 1, 1 - q, nn)
                    for n in staged_at(b, m):
                        stage_high(n)
                    if nn and m == 3:
                        x_out(b + 1, 1 - q, nn)
                    if nn and m == 5:
                        tanh(b + 1, nn)

            schedule(act, body)
            high(NBLK - 1, LAST_NT, NSH - 1)
            store(NBLK - 1, (NBLK - 1) % 2, LAST_NT)
            act.wait_ge(s[f"stored{(NBLK - 1) % 2}"], 8 * (NBLK + 1) + 16)

        @block.gpsimd
        def _(pool):
            nc.gpsimd.memset(mhalf[:], -0.5).then_inc(s["memsets"], 1)
            nc.gpsimd.memset(eps[:], EPS).then_inc(s["memsets"], 1)
            nc.gpsimd.memset(ones[:], 1.0).then_inc(s["memsets"], 1)
            nc.gpsimd.memset(oh[:], 0.0).then_inc(s["memsets"], 1)
            nc.gpsimd.memset(fill[:].bitcast(F32), 0.0).then_inc(s["memsets"], 1)
            pool.wait_ge(s["memsets"], 5)

            def rstd(b, nt):
                pool.wait_ge(s["mv_ready"], b + 1)
                nc.gpsimd.tensor_tensor(ve[:, 0:nt], mv[:, 0:nt, 1:2], eps[:, 0:nt], ALU.add).then_inc(s["ve_ready"], 1)
                pool.wait_ge(s["ve_ready"], b + 1)
                nc.gpsimd.tensor_tensor(rs[:, 0:nt], ve[:, 0:nt], mhalf[:, 0:nt], ALU.pow).then_inc(s["rs_ready"], 1)

            def x_low(b, q, nt):
                pool.wait_ge(s["xhi_ready"], b + 1)
                nc.gpsimd.tensor_tensor(xs[q][:, 0:nt, D:D + 64], xn[:, 0:nt, 128:D], xs[q][:, 0:nt, 128:D], ALU.subtract)
                nc.gpsimd.tensor_tensor(xs[q][:, 0:nt, D + 64:XW], xn[:, 0:nt, 0:128], xs[q][:, 0:nt, 0:128],
                                        ALU.subtract).then_inc(s["xlo_ready"], 1)

            def low(b, nt, m, first=False):
                n = nt * 128
                pool.wait_ge(s["hh_ready"], chunk_sem(b, m) + 1)
                nc.gpsimd.tensor_tensor(hl[m % 2][:, 0:n], hf[m % 2][:, 0:n], hh[m % 2][:, 0:n],
                                        ALU.subtract).then_inc(s["hl_ready"], 1)

            def send(b, q, t):
                if t == 0:
                    pool.wait_ge(s["slots_ready"], b + 1)
                    nc.gpsimd.tensor_tensor(carry[:], eps[:, 0], eps[:, 0], ALU.add)
                for k in range(2):
                    nc.gpsimd.indirect_dma_start(
                        out=routed[:, :], out_offset=bass.IndirectOffsetOnAxis(ap=slot[q][:, k, t:t + 1], axis=0),
                        in_=rows_w[q][:, t, :], in_offset=None, bounds_check=XROWS - 1,
                        oob_is_err=False).then_inc(s[f"sent{q}"], 16)

            rstd(0, NT)
            x_low(0, 0, NT)

            def body(b, q, nt, nn):
                for m in range(NSH):
                    if m >= 1:
                        low(b, nt, m - 1)
                    elif not is_first(b):
                        low(b - 1, NT, NSH - 1)
                    if nn and m == 0:
                        rstd(b + 1, nn)
                    if nn and m == 2:
                        x_low(b + 1, 1 - q, nn)
                    if m < nt:
                        send(b, q, m)

            schedule(pool, body)
            low(NBLK - 1, LAST_NT, NSH - 1)
            pool.wait_ge(s["sent1"], SENT // 2 * (NBLK - 1))
            pool.wait_ge(s["sent0"], SENT // 2 * (NBLK - 1) + 32 * LAST_NT)

        @block.vector
        def _(dve):
            dve.wait_ge(s["memsets"], 5)
            dve.wait_ge(s["const_in"], 112)
            dve.wait_ge(s["wrf_hi"], 2)
            nc.vector.tensor_tensor(wr[1][:], wrf[:], wr[0][:], ALU.subtract).then_inc(s["wr_ready"], 1)

            def add(b, q, nt):
                dve.wait_ge(s[f"rows_in{q}"], 40 * (b - q) + 80)
                if not isinstance(b, int) or b >= 2:
                    dve.wait_ge(s["kept"], b - 1)
                nc.vector.tensor_tensor(h2[q][:, 0:nt], hin[q][:, 0:nt], yin[q][:, 0:nt],
                                        ALU.add).then_inc(s["h2_ready"], 1)
                dve.wait_ge(s["h2_ready"], b + 1)
                for t in range(nt):
                    last = nc.vector.bn_stats(st[:, t], h2[q][:, t])
                last.then_inc(s["stats_ready"], 1)
                dve.wait_ge(s["memsets"], 5)
                dve.wait_ge(s["stats_ready"], b + 1)
                for t in range(nt):
                    last = nc.vector.bn_aggr(mv[:, t], st[:, t])
                last.then_inc(s["mv_ready"], 1)

            def normal(b, q, nt):
                dve.wait_ge(s["rs_ready"], b + 1)
                for t in range(nt):
                    last = nc.vector.tensor_scalar(xn[:, t], h2[q][:, t], mv[:, t, 0:1], rs[:, t], ALU.subtract,
                                                   ALU.mult)
                last.then_inc(s["xn_ready"], 1)

            def step(ins, b, k):
                ins.then_inc(s["route"], 1)
                dve.wait_ge(s["route"], ROUTE * b + k)

            def logits(b, q, nt):
                dve.wait_ge(s["lg_ps"], b + 1)
                src = psx[:, 1, 256:256 + 16 * nt].rearrange("p (t e) -> p t e", e=16)[:, :, 0:E + 1]
                step(nc.vector.scalar_tensor_tensor(out=lg[:, 0:nt], in0=src, scalar=1.0 / SCALE, in1=sgb[:, 0:nt],
                                                    op0=ALU.mult, op1=ALU.add), b, 1)
                nc.vector.tensor_copy(z[:, 0:nt, 1:2], lg[:, 0:nt, E:E + 1])
                for t in range(nt):
                    last = nc.vector.max(m8[:, t], lg[:, t, 0:E])
                step(last, b, 2)
                nc.vector.tensor_tensor(z[:, 0:nt, 0:1], m8[:, 0:nt, 0:1], m8[:, 0:nt, 1:2],
                                        ALU.subtract).then_inc(s["route"], 1)
                for t in range(nt):
                    last = nc.vector.max_index(ix[:, t], m8[:, t], lg[:, t, 0:E])
                step(last, b, 4)
                step(nc.vector.tensor_copy(ixf[:, 0:nt], ix[:, 0:nt, 0:2]), b, 5)
                shape = [128, nt, E]
                for k in range(2):
                    last = nc.vector.tensor_tensor(hot[:, k, 0:nt], iota[:, 0:nt],
                                                   ixf[:, 0:nt, k:k + 1].to_broadcast(shape), ALU.is_equal)
                step(last, b, 6)
                step(nc.vector.tensor_tensor(both[:], hot[:, 0], hot[:, 1], ALU.add), b, 7)
                mask = valid[:, int(nt == LAST_NT)].unsqueeze(2).to_broadcast([128, NT, E])
                nc.vector.tensor_tensor(oh[:, 0:NT], both[:], mask, ALU.mult).then_inc(s["oh_ready"], 1)

            def slots(b, q, nt):
                dve.wait_ge(s["th_ready"], b + 1)
                nc.vector.tensor_scalar(ga[:, 0:nt], th[:, 0:nt], 0.5, 0.5, ALU.mult, ALU.add)
                step(nc.vector.tensor_scalar(gb[:, 0:nt], th[:, 0:nt], -0.5, 0.5, ALU.mult, ALU.add), b, 8)
                nc.vector.tensor_scalar(alpha[q][:, 0:nt], ga[:, 0:nt, 1], 1.0 / SCALE, None, ALU.mult)
                nc.vector.tensor_tensor(gd[:, 0:nt, 0], ga[:, 0:nt, 0], gb[:, 0:nt, 0], ALU.subtract)
                step(nc.vector.tensor_copy(gd[:, 0:nt, 1], gb[:, 0:nt, 0]), b, 9)
                word = words[q][:, 0:nt].bitcast(F32)
                nc.vector.scalar_tensor_tensor(out=word[:, :, 2:4], in0=gd[:, 0:nt], scalar=1.0 / SCALE,
                                               in1=gb[:, 0:nt, 1:2].to_broadcast([128, nt, 2]),
                                               op0=ALU.mult, op1=ALU.mult)
                nc.vector.tensor_copy(word[:, :, 1:2], ixf[:, 0:nt, 0:1])
                at = b * NT if nt == NT else (NBLK - 1) * NT
                nc.vector.tensor_copy(words[q][:, 0:nt, 0:1],
                                      ids[:, bass.ds(at, nt)].unsqueeze(2))
                dve.wait_ge(s["rank_ps"], b + 1)
                step(nc.vector.tensor_tensor(rank[:, 0:nt],
                                             psx[:, 1, 384:384 + nt * E].rearrange("p (t e) -> p t e", e=E),
                                             base[:].unsqueeze(1).to_broadcast([128, nt, E]), ALU.add), b, 10)
                nc.vector.tensor_tensor(base[:], base[:], psx[:, 1, 384 + NT * E:384 + (NT + 1) * E], ALU.add)
                for k in range(2):
                    last = nc.vector.tensor_tensor(pick[:, k, 0:nt], hot[:, k, 0:nt], rank[:, 0:nt], ALU.mult)
                step(last, b, 11)
                for k in range(2):
                    last = nc.vector.tensor_reduce(slotf[:, k, 0:nt], pick[:, k, 0:nt], op=ALU.add,
                                                   axis=mybir.AxisListType.X)
                step(last, b, 12)
                away = far[:, int(nt == LAST_NT)].unsqueeze(1).to_broadcast([128, 2, NT])[:, :, 0:nt]
                step(nc.vector.tensor_tensor(slotf[:, :, 0:nt], slotf[:, :, 0:nt], away, ALU.add), b, 13)
                if not isinstance(b, int) or b >= 2:
                    dve.wait_ge(s[f"sent{q}"], SENT // 2 * (b - q))
                step(nc.vector.tensor_copy(slot[q][:, :, 0:nt], slotf[:, :, 0:nt]), b, 14)
                nc.vector.tensor_copy(ixf[:, 0:nt], ixf[:, 0:nt]).then_inc(s["slots_ready"], 1)

            def unit_table():
                k = [0]

                def step(ins):
                    k[0] += 1
                    ins.then_inc(s["table"], 1)
                    dve.wait_ge(s["table"], k[0])

                X = mybir.AxisListType.X
                nc.vector.tensor_copy(base_u[:], base[:]).then_inc(s["base_ready"], 1)
                step(nc.vector.tensor_tensor(count[:], base[:], const("cap"), ALU.subtract))
                step(nc.vector.tensor_tensor(over[:], count[:].unsqueeze(2).to_broadcast([128, E, NBLK]),
                                             const("thr").unsqueeze(1).to_broadcast([128, E, NBLK]), ALU.is_gt))
                step(nc.vector.tensor_reduce(units[:], over[:], op=ALU.add, axis=X))
                step(nc.vector.tensor_tensor(starts[:], units[:].unsqueeze(1).to_broadcast([128, E + 1, E]),
                                             const("below", "p (a e) -> p a e", e=E), ALU.mult))
                step(nc.vector.tensor_reduce(start[:], starts[:], op=ALU.add, axis=X))
                nc.vector.tensor_copy(jump[:, 0:1], const("starts")[:, 0:1])
                step(nc.vector.scalar_tensor_tensor(out=jump[:, 1:E + 1], in0=units[:], scalar=-float(UNIT),
                                                    in1=const("starts")[:, 1:E + 1], op0=ALU.mult, op1=ALU.add))
                shape = [128, NU, E + 1]
                step(nc.vector.tensor_tensor(ge[:], const("unit").unsqueeze(2).to_broadcast(shape),
                                             start[:].unsqueeze(1).to_broadcast(shape), ALU.is_ge))
                step(nc.vector.tensor_tensor(gj[:], ge[:], jump[:].unsqueeze(1).to_broadcast(shape), ALU.mult))
                nc.vector.tensor_reduce(t["expert"][:], ge[:], op=ALU.add, axis=X)
                step(nc.vector.tensor_reduce(rowf[:], gj[:], op=ALU.add, axis=X))
                step(nc.vector.tensor_scalar(t["expert"][:], t["expert"][:], 1.0, None, ALU.subtract))
                nc.vector.scalar_tensor_tensor(out=rowf[:], in0=const("unit"), scalar=float(UNIT), in1=rowf[:],
                                               op0=ALU.mult, op1=ALU.add)
                step(nc.vector.tensor_scalar(colf[:], t["expert"][:], float(E - 1), None, ALU.min))
                step(nc.vector.tensor_scalar(colf[:], colf[:], float(W_EXPERT), float(W_SHARED), ALU.mult, ALU.add))
                nc.vector.tensor_copy(t["units"][:, 0], rowf[:])
                nc.vector.tensor_copy(t["units"][:, 1], colf[:])
                step(nc.vector.tensor_tensor(pairs2[:], start[:, E:E + 1].to_broadcast([128, NU // 2]),
                                             const("even"), ALU.is_gt))
                step(nc.vector.tensor_reduce(pairf[:], pairs2[:], op=ALU.add, axis=X))
                step(nc.vector.tensor_scalar(pairf[:], pairf[:], 1.0, None, ALU.subtract))
                step(nc.vector.tensor_copy(t["pairs"][:], pairf[:]))

            def hidden(b, nt, m):
                n = nt * 128
                i = m % 2
                dve.wait_ge(s["sg_ready"], chunk_sem(b, m) + 1)
                dve.wait_ge(s["u_ps"], chunk_sem(b, m) + 1)
                if m >= 2 or not is_first(b):
                    dve.wait_ge(s["hl_ready"], chunk_sem(b, m) - 1)
                ins = nc.vector.scalar_tensor_tensor(out=hf[i][:, 0:n], in0=psu[:, i, 0:n], scalar=1.0 / SCALE,
                                                     in1=sg[i][:, 0:n], op0=ALU.mult, op1=ALU.mult)
                ins.then_inc(s["hf_ready"], 1)

            def token_out(b, q, nt):
                dve.wait_ge(s["down"], chunk_sem(b, NSH))
                dve.wait_ge(s["kept"], b + 1)
                for t in range(nt):
                    last = nc.vector.scalar_tensor_tensor(
                        out=ot[q][:, t], in0=pso[:, t // 2, (t % 2) * D:(t % 2 + 1) * D],
                        scalar=alpha[q][:, t:t + 1], in1=ot[q][:, t], op0=ALU.mult, op1=ALU.add)
                last.then_inc(s["out_ready"], 1)

            for i in range(2):
                dve.sem_inc(s[f"stored{i}"], 16)
            nc.vector.tensor_copy(base[:], const("cap")).then_inc(s["base_set"], 1)
            dve.wait_ge(s["base_set"], 1)
            nc.vector.tensor_copy(fill[:, :, XW // 2:XW // 2 + 1],
                                  ids[:, NBLK * NT:(NBLK + 1) * NT].unsqueeze(2)).then_inc(s["fill_ready"], 1)
            def stage_low(n):
                at, width = pieces[n]
                dve.wait_ge(s["stage_hi"], n + 1)
                hi, lo = (x[:, at:at + width] for x in w)
                nc.vector.scalar_tensor_tensor(out=lo, in0=stage[n % 2][:, 0:width], scalar=SCALE, in1=hi,
                                               op0=ALU.mult, op1=ALU.subtract).then_inc(s["stage_lo"], 1)

            for n in range(4):
                stage_low(n)
            add(0, 0, NT)
            normal(0, 0, NT)
            logits(0, 0, NT)
            slots(0, 0, NT)

            def body(b, q, nt, nn):
                for m in range(NSH):
                    hidden(b, nt, m)
                    if nn and m == 0:
                        add(b + 1, 1 - q, nn)
                    if nn and m == 1:
                        normal(b + 1, 1 - q, nn)
                    if m == 1 and not is_first(b):
                        token_out(b - 1, 1 - q, NT)
                    for n in staged_at(b, m):
                        stage_low(n)
                    if nn and m == 4:
                        logits(b + 1, 1 - q, nn)
                    if nn and m == 5:
                        slots(b + 1, 1 - q, nn)

            schedule(dve, body)
            token_out(NBLK - 1, (NBLK - 1) % 2, LAST_NT)
            unit_table()


def routed_experts(nc, t, routed, out):
    with ExitStack() as ctx:
        def sb(name, shape, dt=F32):
            return ctx.enter_context(nc.sbuf_tensor("unit_" + name, shape, dt))

        w, ident = t["w"], t["ident"]
        H1 = HE - 128
        xu = [sb(f"xu{i}", [128, NT, RX // 2], U32) for i in range(2)]
        x16 = [x[:].bitcast(F16) for x in xu]
        xt = [sb(f"xtu{i}", [128, 3, UNIT], F16) for i in range(2)]
        token = [sb(f"token{i}", [128, NT], U32) for i in range(2)]
        tokens = sb("tokens", [128, NU, NT], U32)
        gates = sb("gates", [128, NU, NT])
        gate1 = sb("gate_part", [128, NT])
        sg0 = sb("sg0", [128, UNIT])
        sg1 = sb("sg1", [128, UNIT])
        h0 = [sb(f"h0_{i}", [128, UNIT]) for i in range(2)]
        h1 = [sb(f"h1_{i}", [128, UNIT]) for i in range(2)]
        h0h = [sb(f"h0h{i}", [128, UNIT], F16) for i in range(2)]
        h0l = [sb(f"h0l{i}", [128, UNIT], F16) for i in range(2)]
        h1s = [sb(f"h1s{i}", [128, UNIT], F16) for i in range(2)]
        const = sb("const", [128, 1])
        carry = sb("carry", [128, 2])
        y = [sb(f"yu{i}", [128, NT, D]) for i in range(2)]
        psg = ctx.enter_context(nc.psum_tensor("u_gate", [128, 512], F32))
        psu = ctx.enter_context(nc.psum_tensor("u_up", [128, 512], F32))
        psc = ctx.enter_context(nc.psum_tensor("u_short", [128, 512], F32))
        psx = ctx.enter_context(nc.psum_tensor("u_turn", [128, 2, 512], F32))
        pso = ctx.enter_context(nc.psum_tensor("u_out", [128, 2, 512], F32))
        px16 = [psx[:, i].bitcast(F16) for i in range(2)]
        names = ("x_in0", "x_in1", "xt_ps", "xt_d", "xt_a", "gate1_ready", "meta", "g_ps", "u_ps", "c_ps", "sg0_ready",
                 "sg1_ready", "h0_ready", "h1_ready", "h0h_ready", "h0l_ready", "h1h_ready", "h1l_ready", "down",
                 "y_a", "y_d", "added", "begun", "turn", "token_ready", "const_ready")
        s = {name: ctx.enter_context(nc.semaphore("r_" + name)) for name in names}
        block = ctx.enter_context(nc.Block())

        def pairs(eng):
            return eng.value_load(t["pairs"][0:1, 0:1], min_val=MIN_UNITS // 2 - 1,
                                  max_val=(MAX_UNITS + 1) // 2 - 1) + 1

        def schedule(n, eng, body):
            for i in range(2):
                body(i, i)
            with eng.Fori(1, n) as j:
                for i in range(2):
                    body(2 * j + i, i)

        def table(eng, row, i):
            lo, hi = ((0, XROWS - UNIT), (W_SHARED, W_SHARED + (E - 1) * W_EXPERT))[row]
            return eng.value_load(t["units"][0:1, row, bass.ds(i, 1)], min_val=lo, max_val=hi)

        def wait(eng, name, value):
            if not (isinstance(value, int) and value <= 0):
                eng.wait_ge(s[name], value)

        @block.sync
        def _(sp):
            n = pairs(nc.sync)

            def load(i, q):
                wait(sp, "xt_ps", 2 * (i - 1))
                wait(sp, "meta", i - 1)
                at = table(nc.sync, 0, i)
                sp.dma_start(xu[q][:], routed[bass.ds(at, UNIT)].rearrange("(t p) d -> p t d", p=128)
                             ).then_inc(s[f"x_in{q}"], 16)

            schedule(n, sp, load)
            load(2 * n, 0)

        @block.tensor
        def _(pe):
            n = pairs(nc.tensor)
            pe.wait_ge(s["begun"], 1)

            def transposes(i, q):
                pe.wait_ge(s[f"x_in{q}"], 8 * (i - q) + 16)
                wait(pe, "xt_d", i)
                wait(pe, "xt_a", i)
                for c in range(3):
                    for k in range(NT):
                        o = px16[c // 2][:, (c % 2) * UNIT + k * 128:(c % 2) * UNIT + (k + 1) * 128]
                        last = nc.tensor.transpose(o, x16[q][:, k, c * 128:(c + 1) * 128], ident[:])
                    if c:
                        last.then_inc(s["xt_ps"], 1)

            def up(i, q):
                col = table(nc.tensor, 1, i)
                pe.wait_ge(s["xt_d"], i + 1)
                pe.wait_ge(s["xt_a"], i + 1)
                wait(pe, "h0_ready", i)
                wait(pe, "h1_ready", i)
                pe.wait_ge(s["begun"], 1)
                for k, (ps, done) in enumerate(((psg, "g_ps"), (psu, "u_ps"), (psc, "c_ps"))):
                    a, b = k * 128, 2 * HE + k * 128
                    prods = ((0, a, 0), (1, a, 0), (0, a, 2), (0, b, 1), (1, b, 1))
                    for m, (part, off, c) in enumerate(prods):
                        last = nc.tensor.matmul(ps[:], w[part][:, bass.ds(col + off, 128)], xt[q][:, c],
                                                start=(m == 0), stop=(m == 4))
                    last.then_inc(s[done], 1)

            def down(i, q):
                col = table(nc.tensor, 1, i)
                wait(pe, "y_d", i)
                wait(pe, "y_a", i)
                pe.wait_ge(s["h0l_ready"], i + 1)
                pe.wait_ge(s["h1l_ready"], i + 1)
                pe.wait_ge(s["begun"], 1)
                prods = ((h0h, 0, 4 * HE), (h0h, 1, 4 * HE), (h0l, 0, 4 * HE), (h1s, 0, 4 * HE + D),
                         (h1s, 1, 4 * HE + D))
                for k in range(NT):
                    o = pso[:, k // 2, (k % 2) * D:(k % 2 + 1) * D]
                    for m, (h, part, off) in enumerate(prods):
                        last = nc.tensor.matmul(o, h[q][:, k * 128:(k + 1) * 128],
                                                w[part][:, bass.ds(col + off, D)],
                                                start=(m == 0 and k % 2 == 0), stop=(m == 4), skip_group_check=True)
                last.then_inc(s["down"], 1)

            transposes(0, 0)

            def body(i, q):
                up(i, q)
                transposes(i + 1, 1 - q)
                if not (isinstance(i, int) and i == 0):
                    down(i - 1, 1 - q)

            schedule(n, pe, body)
            down(2 * n - 1, 1)

        @block.scalar
        def _(act):
            n = pairs(nc.scalar)
            S = slice(128 - H1, 128)

            def x_out(i, q):
                act.wait_ge(s["xt_ps"], 2 * i + 2)
                nc.scalar.copy(xt[q][:, 2], px16[1][:, 0:UNIT]).then_inc(s["xt_a"], 1)

            def y_out(i, q):
                act.wait_ge(s["down"], i + 1)
                wait(act, "turn", i)
                act.wait_ge(s["meta"], i + 1)
                for k in range(2, NT):
                    last = nc.scalar.mul(y[q][:, k], pso[:, 1, (k - 2) * D:(k - 1) * D], gates[:, bass.ds(i, 1), k])
                last.then_inc(s["y_a"], 1)

            x_out(0, 0)

            def body(i, q):
                act.wait_ge(s["g_ps"], i + 1)
                wait(act, "h0_ready", i)
                nc.scalar.activation(sg0[:], psg[:], ACT.Silu, scale=1.0 / SCALE).then_inc(s["sg0_ready"], 1)
                act.wait_ge(s["c_ps"], i + 1)
                wait(act, "h1_ready", i)
                nc.scalar.activation(sg1[S], psc[0:H1], ACT.Silu, scale=1.0 / SCALE).then_inc(s["sg1_ready"], 1)
                act.wait_ge(s["h0_ready"], i + 1)
                wait(act, "down", i - 1)
                nc.scalar.copy(h0h[q][:], h0[q][:]).then_inc(s["h0h_ready"], 1)
                x_out(i + 1, 1 - q)
                act.wait_ge(s["h1_ready"], i + 1)
                nc.scalar.copy(h1s[q][S], h1[q][S]).then_inc(s["h1h_ready"], 1)
                if not (isinstance(i, int) and i == 0):
                    y_out(i - 1, 1 - q)

            schedule(n, act, body)
            y_out(2 * n - 1, 1)

        @block.gpsimd
        def _(pool):
            n = pairs(nc.gpsimd)

            def add(i, q):
                pool.wait_ge(s["meta"], i + 1)
                nc.gpsimd.tensor_tensor(carry[:, 0:1], const[:], const[:], ALU.add)
                nc.gpsimd.tensor_copy(token[q][:].unsqueeze(1), tokens[:, bass.ds(i, 1)]
                                      ).then_inc(s["token_ready"], 1)
                pool.wait_ge(s["token_ready"], i + 1)
                pool.wait_ge(s["y_a"], i + 1)
                pool.wait_ge(s["y_d"], i + 1)
                wait(pool, "added", 64 * i)
                wait(pool, "turn", i)
                nc.gpsimd.tensor_tensor(carry[:, 1:2], const[:], const[:], ALU.add).then_inc(s["turn"], 1)
                for k in range(NT):
                    nc.gpsimd.indirect_dma_start(
                        out=out[:, :], out_offset=bass.IndirectOffsetOnAxis(ap=token[q][:, k:k + 1], axis=0),
                        in_=y[q][:, k, :], in_offset=None, compute_op=ALU.add).then_inc(s["added"], 16)

            def body(i, q):
                pool.wait_ge(s["h0h_ready"], i + 1)
                nc.gpsimd.tensor_tensor(h0l[q][:], h0[q][:], h0h[q][:], ALU.subtract).then_inc(s["h0l_ready"], 1)
                if not (isinstance(i, int) and i == 0):
                    add(i - 1, 1 - q)

            nc.gpsimd.memset(const[:], 0.0).then_inc(s["const_ready"], 1)
            pool.wait_ge(s["const_ready"], 1)
            schedule(n, pool, body)
            add(2 * n - 1, 1)
            pool.wait_ge(s["added"], 128 * n)

        @block.vector
        def _(dve):
            n = pairs(nc.vector)
            S = slice(128 - H1, 128)

            def meta(i, q):
                dve.wait_ge(s[f"x_in{q}"], 8 * (i - q) + 16)
                wait(dve, "meta", i)
                word = xu[q][:, :, XW // 2:RX // 2].bitcast(F32)
                nc.vector.scalar_tensor_tensor(out=gate1[:].unsqueeze(2), in0=word[:, :, 1:2],
                                               scalar=t["expert"][:, bass.ds(i, 1)], in1=word[:, :, 2:3],
                                               op0=ALU.is_equal, op1=ALU.mult).then_inc(s["gate1_ready"], 1)
                dve.wait_ge(s["gate1_ready"], i + 1)
                nc.vector.tensor_tensor(gates[:, bass.ds(i, 1)], gate1[:].unsqueeze(1),
                                        word[:, :, 3:4].rearrange("p t o -> p o t"), ALU.add)
                nc.vector.tensor_copy(tokens[:, bass.ds(i, 1)],
                                      xu[q][:, :, XW // 2:XW // 2 + 1].rearrange("p t o -> p o t")
                                      ).then_inc(s["meta"], 1)

            def x_out(i, q):
                dve.wait_ge(s["xt_ps"], 2 * i + 1)
                nc.vector.tensor_copy(xt[q][:, 0:2], px16[0][:, 0:2 * UNIT].rearrange("p (c n) -> p c n", c=2)
                                      ).then_inc(s["xt_d"], 1)

            def y_out(i, q):
                dve.wait_ge(s["down"], i + 1)
                wait(dve, "turn", i)
                dve.wait_ge(s["meta"], i + 1)
                for k in range(2):
                    last = nc.vector.tensor_scalar(y[q][:, k], pso[:, 0, k * D:(k + 1) * D], gates[:, bass.ds(i, 1), k], None,
                                                   ALU.mult)
                last.then_inc(s["y_d"], 1)

            dve.sem_inc(s["begun"], 1)
            meta(0, 0)
            x_out(0, 0)

            def body(i, q):
                dve.wait_ge(s["sg0_ready"], i + 1)
                dve.wait_ge(s["u_ps"], i + 1)
                wait(dve, "h0l_ready", i - 1)
                nc.vector.scalar_tensor_tensor(out=h0[q][:], in0=psu[:], scalar=1.0 / SCALE, in1=sg0[:], op0=ALU.mult,
                                               op1=ALU.mult).then_inc(s["h0_ready"], 1)
                dve.wait_ge(s["sg1_ready"], i + 1)
                nc.vector.scalar_tensor_tensor(out=h1[q][S], in0=psc[S], scalar=1.0 / SCALE, in1=sg1[S],
                                               op0=ALU.mult, op1=ALU.mult).then_inc(s["h1_ready"], 1)
                x_out(i + 1, 1 - q)
                meta(i + 1, 1 - q)
                dve.wait_ge(s["h1h_ready"], i + 1)
                nc.vector.tensor_tensor(h1s[q][0:H1], h1[q][S], h1s[q][S], ALU.subtract).then_inc(s["h1l_ready"], 1)
                if not (isinstance(i, int) and i == 0):
                    y_out(i - 1, 1 - q)

            schedule(n, dve, body)
            y_out(2 * n - 1, 1)


def build(nc, io, out):
    taps = nc.dram_tensor("taps", (D, RW, 2), F16, kind="Internal").ap()
    resid = nc.dram_tensor("resid", (NTOK, D), F32, kind="Internal").ap()
    mixed = nc.dram_tensor("mixed", (4, NTOK, DQ), F32, kind="Internal").ap()
    routed = nc.dram_tensor("routed", (XROWS, RX // 2), U32, kind="Internal").ap()
    with ExitStack() as outer:
        y_stored = outer.enter_context(nc.semaphore("y_stored"))
        area = outer.enter_context(nc.sbuf_tensor("area", [128, AREA], F32))
        with ExitStack() as ctx:
            u = [ctx.enter_context(nc.sbuf_tensor(f"u{i}", [HALF + 1, 2, DH, 2, B], F16)) for i in range(2)]
            with ExitStack() as emb:
                w = {"hi": emb.enter_context(nc.sbuf_tensor("w_hi", [ROWS, C, D], F16)),
                     "lo": emb.enter_context(nc.sbuf_tensor("w_lo", [ROWS, C, D], F16)),
                     "x": emb.enter_context(nc.sbuf_tensor("w_x", [NX, D], F16)),
                     "signs": emb.enter_context(nc.sbuf_tensor("signs", [NX, 2], F32)),
                     "xe": [emb.enter_context(nc.sbuf_tensor(f"xe{i}", [NX, GT], F32)) for i in range(2)],
                     "x_in": [emb.enter_context(nc.semaphore(f"x_in{i}")) for i in range(2)]}
                load_signs(nc, io, w)
                prepare(nc, io, u, w, area, (taps, resid, mixed))
                embed(nc, io, u, w, area, resid)
            mix(nc, u, area, y_stored, taps, mixed)
        feed_forward(nc, io, area, y_stored, resid, mixed, routed, out)


def load_signs(nc, io, w):
    with nc.semaphore("signs_in") as signs_in, nc.Block() as block:
        @block.sync
        def _(sp):
            sp.dma_start(w["signs"][:], io["signs"][:]).then_inc(signs_in, 16)
            sp.wait_ge(signs_in, 16)


def constants():
    fa, fx = dft_constants()
    signs = np.zeros((NX, 2), np.float32)
    signs[6:12, 0] = -1.0
    signs[12:18, 1] = -1.0
    iota = np.broadcast_to(np.arange(E, dtype=np.float32), (128, NT, E))
    slot = np.arange(NT)[None] * 128 + np.arange(128)[:, None]
    ids = [b * BT + slot for b in range(NBLK - 1)] + [LAST_START + slot, NTOK + slot]
    return {"fa": fa, "fx": fx, "signs": signs, "iota": np.ascontiguousarray(iota),
            "ids": np.concatenate(ids, 1).astype(np.uint32), "ctab": table_constants(),
            "ident": np.eye(128, dtype=np.float16), "tri": np.triu(np.ones((128, 128)), 1).astype(np.float16)}


def table_fields():
    widths = (("valid", 2 * NT), ("far", 2 * NT), ("cap", E), ("starts", E + 1), ("thr", NBLK), ("unit", NU),
              ("below", (E + 1) * E), ("even", NU // 2))
    fields, at = {}, 0
    for name, width in widths:
        fields[name] = (at, width)
        at += width
    return fields, at


def table_constants():
    fields, total = table_fields()
    t = np.zeros((128, total), np.float32)
    old = NBLK * BT - BT - LAST_START
    valid = np.ones((128, 2, NT), np.float32)
    valid[:old, 1, 0] = 0.0
    far = (1.0 - valid) * XROWS
    valid[:, 1, LAST_NT:] = 0.0
    values = {"valid": valid.reshape(128, -1), "far": far.reshape(128, -1), "cap": np.arange(E) * CAP,
              "starts": np.r_[0, np.full(E, CAP)], "thr": np.arange(NBLK) * UNIT, "unit": np.arange(NU),
              "below": np.tril(np.ones((E + 1, E)), -1).reshape(-1), "even": 2 * np.arange(NU // 2)}
    for name, (at, width) in fields.items():
        t[:, at:at + width] = values[name]
    return t


def layout(inputs):
    g = {k.replace("L0_", ""): np.asarray(v) for k, v in inputs.items()}
    first, second, _, rest = pixel_fold()
    x = g["x"].reshape(B, C, SIDE, P, SIDE, P).transpose(1, 3, 5, 0, 2, 4).reshape(C, P * P, NG, GT)

    def pick(pix):
        return x[:, [r * P + s for r, s in pix]]

    a = {"xa": pick(first).transpose(2, 1, 0, 3), "xb": pick(second).transpose(2, 1, 0, 3)}
    rest = pick(rest).transpose(2, 0, 1, 3).reshape(NG, 2 * C, GT)
    a["xe"] = np.tile(rest, (1, 3, 1))
    a["pw"] = g["tok_proj_w"].T.reshape(C, 2, FCH, D).transpose(2, 1, 0, 3)
    wh = np.repeat(g["tok_freq_weight_h"], KW).reshape(2, FCH)
    ww = np.tile(g["tok_freq_weight_w"], KH).reshape(2, FCH)
    a["freq"] = np.stack([wh, ww]).transpose(2, 0, 1)
    pos = g["tok_position_embeddings"][0]
    bias = np.broadcast_to(g["tok_proj_b"], (HALF, 2, D))
    a["pos"] = np.stack([bias, pos[1:].reshape(2, HALF, D).transpose(1, 0, 2)])
    a["cls"] = np.broadcast_to(np.stack([g["tok_cls_token"][0, 0], pos[0]]), (3, 2, D))

    def states(m):
        m = m.reshape(2, 2, NCG // 2, CG // 2, NST).transpose(0, 4, 2, 1, 3)
        return m.reshape(128, DH)

    delta = np.broadcast_to(g["attn_delta"][:, None], (D, NST))
    a["ssm"] = np.stack([states(m) for m in (g["attn_A_re"], g["attn_A_im"], g["attn_B_mat"], g["attn_C_mat"], delta)], 1)
    cols = []

    def add_columns(m):
        cols.extend([m[0:128], np.concatenate([m[128:D], m[128:D]], 0)])

    add_columns(np.concatenate([g["ffn_ws_gate"], g["ffn_ws_up"]], 1))
    cols.append(g["ffn_ws_down"].reshape(NSH, 128, D).transpose(1, 0, 2).reshape(128, NSH * D))
    for e in range(E):
        wg, wu = g["ffn_w_gate"][e], g["ffn_w_up"][e]
        add_columns(np.concatenate([wg[:, 0:128], wu[:, 0:128], wg[:, 128:HE], wu[:, 128:HE]], 1))
        add_columns(g["ffn_w_down"][e])
    a["w_all"] = np.concatenate(cols, 1)
    r = np.concatenate([g["ffn_router_w"], g["ffn_sg_w"]], 1)
    a["w_r"] = np.stack([r[0:128], np.concatenate([r[128:D], r[128:D]], 0)], 1)
    sgb = np.zeros((128, NT, E + 1), np.float32)
    sgb[:, :, E] = g["ffn_sg_b"][0]
    a["sgb"] = sgb
    a.update(constants())
    return {k: np.ascontiguousarray(v) for k, v in a.items()}


def kernel(**inputs):
    import concourse.bacc as _bacc
    from concourse import mybir as _mybir
    from concourse.bass_utils import run_bass_kernel_spmd as _run

    nc = _bacc.Bacc("TRN2", target_bir_lowering=False, num_devices=1)
    arrays, io = {}, {}
    for name, a in layout(inputs).items():
        arrays[f"in_{name}_dram"] = a
        io[name] = nc.dram_tensor(f"in_{name}_dram", a.shape, _mybir.dt.from_np(a.dtype), kind="ExternalInput").ap()
    out = nc.dram_tensor("out_0_dram", (OUT_ROWS, D), _mybir.dt.float32, kind="ExternalOutput").ap()
    build(nc, io, out)
    r = _run(nc, [arrays], core_ids=[0])
    return r.results[0]["out_0_dram"][:NTOK].reshape(B, SEQ, D)
```
